# Optimizing a Trainium2 kernel written in Bass

```python
import numpy as np
import jax
import jax.numpy as jnp

def _softmax(x, axis=-1):
    return jax.nn.softmax(x, axis=axis)

def _gelu(x):
    return jax.nn.gelu(x, approximate=True)

def _silu(x):
    return jax.nn.silu(x)

def _sigmoid(x):
    return jax.nn.sigmoid(x)

def _layernorm(x, axis=-1, eps=1e-05):
    m = jnp.mean(x, axis=axis, keepdims=True)
    v = jnp.var(x, axis=axis, keepdims=True)
    return (x - m) / jnp.sqrt(v + eps)

def _scatter_add(tgt, idx, src, axis=0):
    return tgt.at[idx].add(src)

def _segment_sum(src, seg, n):
    return jax.ops.segment_sum(src, seg, n)
kernel_name = 'mk_prb_d1_jaxref_r4_2ace6d'

def setup_inputs(seed: int=0):
    np.random.seed(seed)
    _w = jnp.asarray

    def _L0_attn_setup():
        import jax, jax.numpy as jnp
        import numpy as np
        HEADS = 16
        DIM_HEAD = 64
        SEG = 128
        P = 16

        def rmsnorm(x, g, eps=1e-06):
            var = jnp.mean(x * x, axis=-1, keepdims=True)
            return x * jax.lax.rsqrt(var + eps) * g
        key = jax.random.key(seed)
        ks = jax.random.split(key, 6)
        B, S, D = (2, 1024, 256)
        inner = HEADS * DIM_HEAD
        return {'x': jax.random.normal(ks[0], (B, S, D), jnp.float32), 'gamma': jnp.ones((D,), jnp.float32), 'w_qkv': jax.random.normal(ks[1], (D, inner * 3), jnp.float32) * D ** (-0.5), 'w_out': jax.random.normal(ks[2], (inner, D), jnp.float32) * inner ** (-0.5), 'pm_k': jax.random.normal(ks[3], (HEADS, P, DIM_HEAD), jnp.float32) * 0.02, 'pm_v': jax.random.normal(ks[4], (HEADS, P, DIM_HEAD), jnp.float32) * 0.02}
    _L0_attn_in = _L0_attn_setup()

    def _L0_ffn_setup():
        import jax, jax.numpy as jnp
        import numpy as np
        B, T, D = (2, 256, 256)
        H, DK, K = (8, 128, 8)
        NKEYS = 64
        NEXP = NKEYS * NKEYS

        def _rmsnorm(x, w, eps=1e-06):
            inv = jax.lax.rsqrt(jnp.mean(x * x, axis=-1, keepdims=True) + eps)
            return x * inv * w
        key = jax.random.key(seed)
        ks = jax.random.split(key, 5)
        return {'x': jax.random.normal(ks[0], (B, T, D), jnp.float32), 'w_q': jax.random.normal(ks[1], (H * 2 * DK, D), jnp.float32) * 0.02, 'keys': jax.random.normal(ks[2], (H, NKEYS, 2, DK), jnp.float32) * 0.02, 'expert_down': jax.random.normal(ks[3], (NEXP, D), jnp.float32) * 0.02, 'expert_up': jax.random.normal(ks[4], (NEXP, D), jnp.float32) * 0.02, 'norm_w': jnp.ones((D,), jnp.float32)}
    _L0_ffn_in = _L0_ffn_setup()
    _d = {'L0_attn_x': _L0_attn_in['x'], 'L0_attn_gamma': _L0_attn_in['gamma'], 'L0_attn_w_qkv': _L0_attn_in['w_qkv'], 'L0_attn_w_out': _L0_attn_in['w_out'], 'L0_attn_pm_k': _L0_attn_in['pm_k'], 'L0_attn_pm_v': _L0_attn_in['pm_v'], 'L0_ffn_w_q': _L0_ffn_in['w_q'], 'L0_ffn_keys': _L0_ffn_in['keys'], 'L0_ffn_expert_down': _L0_ffn_in['expert_down'], 'L0_ffn_expert_up': _L0_ffn_in['expert_up'], 'L0_ffn_norm_w': _L0_ffn_in['norm_w']}
    _x0 = _d['L0_attn_x']
    _d['L0_attn_x'] = jax.random.normal(jax.random.fold_in(jax.random.key(seed), 1), (2, 2048, 256), dtype=_x0.dtype)
    del _x0
    return _d

def reference(L0_attn_x, L0_attn_gamma, L0_attn_w_qkv, L0_attn_w_out, L0_attn_pm_k, L0_attn_pm_v, L0_ffn_w_q, L0_ffn_keys, L0_ffn_expert_down, L0_ffn_expert_up, L0_ffn_norm_w):

    def _L0_attn_ref(x, gamma, w_qkv, w_out, pm_k, pm_v):
        import jax, jax.numpy as jnp
        import numpy as np
        HEADS = 16
        DIM_HEAD = 64
        SEG = 128
        P = 16

        def rmsnorm(x, g, eps=1e-06):
            var = jnp.mean(x * x, axis=-1, keepdims=True)
            return x * jax.lax.rsqrt(var + eps) * g
        B, S, D = x.shape
        pad = -S % SEG
        Sp = S + pad
        nw = Sp // SEG
        h = rmsnorm(x, gamma)
        qkv = h @ w_qkv
        q, k, v = jnp.split(qkv, 3, axis=-1)

        def fold(t):
            t = jnp.pad(t, ((0, 0), (0, pad), (0, 0)))
            t = t.reshape(B, nw, SEG, HEADS, DIM_HEAD)
            return t.transpose(0, 1, 3, 2, 4)
        q, k, v = (fold(q), fold(k), fold(v))
        pmk = jnp.broadcast_to(pm_k, (B, nw, HEADS, P, DIM_HEAD))
        pmv = jnp.broadcast_to(pm_v, (B, nw, HEADS, P, DIM_HEAD))
        k = jnp.concatenate([pmk, k], axis=3)
        v = jnp.concatenate([pmv, v], axis=3)
        scale = DIM_HEAD ** (-0.5)
        sim = jnp.einsum('bwhid,bwhjd->bwhij', q, k) * scale
        qi = jnp.arange(SEG)[:, None]
        kj = jnp.arange(SEG + P)[None, :] - P
        mask = (kj < 0) | (qi >= kj)
        sim = jnp.where(mask, sim, -jnp.inf)
        attn = jax.nn.softmax(sim, axis=-1)
        out = jnp.einsum('bwhij,bwhjd->bwhid', attn, v)
        out = out.transpose(0, 1, 3, 2, 4).reshape(B, Sp, HEADS * DIM_HEAD)
        out = out[:, :S]
        return out @ w_out

    def _L0_ffn_ref(x, w_q, keys, expert_down, expert_up, norm_w):
        import jax, jax.numpy as jnp
        import numpy as np
        B, T, D = (2, 256, 256)
        H, DK, K = (8, 128, 8)
        NKEYS = 64
        NEXP = NKEYS * NKEYS

        def _rmsnorm(x, w, eps=1e-06):
            inv = jax.lax.rsqrt(jnp.mean(x * x, axis=-1, keepdims=True) + eps)
            return x * inv * w
        b, t, d = x.shape
        xn = _rmsnorm(x, norm_w)
        q = (xn @ w_q.T).reshape(b, t, H, 2, DK)
        sim1 = jnp.einsum('bthd,hkd->bthk', q[..., 0, :], keys[:, :, 0, :])
        sim2 = jnp.einsum('bthd,hkd->bthk', q[..., 1, :], keys[:, :, 1, :])
        s1, i1 = jax.lax.top_k(sim1, K)
        s2, i2 = jax.lax.top_k(sim2, K)
        all_idx = (i1[..., :, None] * NKEYS + i2[..., None, :]).reshape(b, t, H, K * K)
        all_sc = (s1[..., :, None] + s2[..., None, :]).reshape(b, t, H, K * K)
        fs, pk = jax.lax.top_k(all_sc, K)
        fi = jnp.take_along_axis(all_idx, pk, axis=-1)
        wd = expert_down[fi]
        wu = expert_up[fi]
        hidden = jax.nn.gelu(jnp.einsum('btd,bthkd->bthk', xn, wd), approximate=False)
        hidden = hidden * jax.nn.relu(fs)
        return jnp.einsum('bthk,bthkd->btd', hidden, wu)
    x = L0_attn_x
    xn = _layernorm(x, axis=-1)
    x = x + _L0_attn_ref(xn, L0_attn_gamma, L0_attn_w_qkv, L0_attn_w_out, L0_attn_pm_k, L0_attn_pm_v) + _L0_ffn_ref(xn, L0_ffn_w_q, L0_ffn_keys, L0_ffn_expert_down, L0_ffn_expert_up, L0_ffn_norm_w)
    return x

_drawn_inputs = setup_inputs


def setup_inputs(seed=0):
    import zlib

    import numpy as np

    out = dict(_drawn_inputs(seed))
    spreads = {'L0_attn_gamma': (1.0, 0.6), 'L0_ffn_norm_w': (1.0, 0.6)}
    factors = {'L0_attn_pm_k': 64.0,
     'L0_attn_pm_v': 200.0,
     'L0_ffn_w_q': 6.012,
     'L0_ffn_keys': 5.944,
     'L0_ffn_expert_down': 6.048,
     'L0_ffn_expert_up': 5.892,
     'L0_attn_w_qkv': 8.0,
     'L0_attn_w_out': 8.0}
    for name, (base, spread) in spreads.items():
        noise = np.random.default_rng([zlib.crc32(name.encode()), seed]).standard_normal(out[name].shape)
        drawn = base * np.exp(spread * noise) if base else spread * noise
        out[name] = jnp.asarray(drawn.astype(out[name].dtype))
    for name, factor in factors.items():
        out[name] = (out[name] * factor).astype(out[name].dtype)
    return out
```

```python
from contextlib import ExitStack

import concourse.bass as bass
from concourse import mybir

ALU = mybir.AluOpType
ACT = mybir.ActivationFunctionType
AX = mybir.AxisListType
F32 = mybir.dt.float32
F32R = mybir.dt.float32r
BF16 = mybir.dt.bfloat16
U32 = mybir.dt.uint32

P = 128
BANK = 512
SEG = 128
W = 2
BLK = W * SEG
TOP = 8


def attention_experts(nc, x, gamma, w_qkv, w_out, pm_k, pm_v, w_q, keys, expert_down, expert_up, norm_w, out):
    B, S, D = x.shape
    HEADS, PM, DH = pm_k.shape
    EH, NK, _, DK = keys.shape
    INNER = HEADS * DH
    NEXP = expert_down.shape[0]
    KD = D // P
    NI = B * S // BLK
    CH = INNER // P
    KJ = PM + SEG
    NG = W * HEADS // 4
    HS = EH * 2
    NC = EH * TOP
    LO = NEXP // P
    assert D == 256 and DH == 64 and HEADS == 16 and KJ * 2 <= BANK and NC == 64 and LO == 32 and NK == 64
    assert DK == P and PM * 8 == P
    ROOT = float(DH) ** -0.5

    x_blk = x.rearrange("b s d -> (b s) d").rearrange("(n w p) d -> n p w d", w=W, p=P)
    out_blk = out.rearrange("b s d -> (b s) d").rearrange("(n w p) d -> n p w d", w=W, p=P)
    z_scratch = nc.dram_tensor("z_scratch", [NI, P, 2 * KD * BLK], F32, kind="Internal").ap()
    tab_scratch = nc.dram_tensor("tab_scratch", [W * (NI + 1), P, 3 * 64], F32, kind="Internal").ap()

    with ExitStack() as whole:
        def sem(name):
            return whole.enter_context(nc.semaphore(name))

        def shared(name, shape, dt):
            return whole.enter_context(nc.sbuf_tensor(name, shape, dt))

        ident = shared("ident", [P, P], F32)
        identb = shared("identb", [P, P], BF16)
        gam = shared("gam", [P, KD], F32)
        nrm = shared("nrm", [P, KD], F32)
        upw = shared("upw", [P, LO, D], F32)
        raw = upw[:].rearrange("p a b -> p (a b)")

        c_ident = sem("c_ident")
        c_mask = sem("c_mask")
        c_iota = sem("c_iota")
        d_small = sem("d_small")

        with ExitStack() as ctx:
            def sb(name, shape, dt):
                return ctx.enter_context(nc.sbuf_tensor(name, shape, dt))

            def ps(name, shape, dt=F32):
                return ctx.enter_context(nc.psum_tensor(name, shape, dt))

            maskneg = sb("maskneg", [P, KJ], BF16)
            iota8 = sb("iota8", [P, TOP], F32)
            minus_half = sb("minus_half", [P, W], F32)
            eps = sb("eps", [P, 2, W], F32)
            one = sb("one", [P, 1], F32)
            wqkv_h = sb("wqkv_h", [P, KD, 3 * INNER], F32R)
            wqkv_l = sb("wqkv_l", [P, KD, 3 * INNER], F32R)
            wsc_h = sb("wsc_h", [P, KD, HS * NK], F32R)
            wsc_l = sb("wsc_l", [P, KD, HS * NK], F32R)
            wout = sb("wout", [P, CH, D], F32)
            pmk2 = sb("pmk2", [P, 2, 2 * DH], F32)
            pmv_bd = sb("pmv_bd", [P, 2, 8 * DH], F32)
            xin = sb("xin", [P, W, D], F32)
            xres = sb("xres", [P, W, D], F32)
            stats = sb("stats", [P, W, 6], F32)
            mv = sb("mv", [P, W, 2], F32)
            rr = sb("rr", [P, 6, W], F32)
            z = sb("z", [P, W, D], F32)
            zhl = sb("zhl", [P, 2, KD, BLK], F32R)
            qT = sb("qT", [P, CH, BLK], F32)
            kT = sb("kT", [P, CH, W, KJ], F32)
            v = sb("v", [P, W, INNER], F32)
            sc = sb("sc", [P, W, HS * NK], F32)
            prob = [sb(f"prob{n}", [P, 8, KJ], F32) for n in range(2)]
            probT = [sb(f"probT{n}", [P, 4, P], F32) for n in range(2)]
            probpm = sb("probpm", [P, 2, 8, PM], F32)
            pmT = sb("pmT", [P, 2, P], F32)
            negmax = sb("negmax", [P, NG, 2, 2], F32)
            rowsum = sb("rowsum", [P, NG, 4], F32)
            recip = sb("recip", [P, 8], F32)
            o = sb("o", [P, INNER], F32)
            oT = sb("oT", [P, CH, P], F32)
            y = sb("y", [P, W, D], F32)
            top = sb("top", [P, HS, TOP], F32)
            topi = sb("topi", [P, HS, TOP], U32)
            topf = sb("topf", [P, HS, TOP], F32)
            cand = sb("cand", [P, EH, TOP, TOP], F32)
            best = sb("best", [P, NC], F32)
            besti = sb("besti", [P, NC], U32)
            rank = sb("rank", [P, 2, NC], U32)
            pick = sb("pick", [P, NC, TOP], F32)
            prod = sb("prod", [P, NC, TOP], F32)
            keyi = sb("keyi", [P, 2, NC], F32)
            high = sb("high", [P, NC], F32)
            tab = sb("tab", [P, W, 3, 2, NC], F32)
            tabT = sb("tabT", [P, W, 3, NC], F32)

            aux = [ps(f"aux{n}", [P, BANK]) for n in range(2)]
            sim = [ps(f"sim{n}", [P, 2, BANK]) for n in range(2)]
            ptb = ps("ptb", [P, 4, P])
            pvb = ps("pvb", [P, BANK])

            d_raw = sem("d_raw")
            d_wq = sem("d_wq")
            d_pmv = sem("d_pmv")
            d_wout = sem("d_wout")
            c_pmv0 = sem("c_pmv0")
            c_roots = sem("c_roots")
            set_ps = sem("set_ps")
            set_ev = sem("set_ev")
            w_hi = sem("w_hi")
            w_split = sem("w_split")
            d_xin = sem("d_xin")
            d_xres = sem("d_xres")
            st_z = sem("st_z")
            st_tab = [sem(f"st_tab{w}") for w in range(W)]
            st_y = [sem(f"st_y{w}") for w in range(W)]
            ln_bn = sem("ln_bn")
            ln_mv = sem("ln_mv")
            ln_step = sem("ln_step")
            ln_r = sem("ln_r")
            z_ready = sem("z_ready")
            z_hi = sem("z_hi")
            aux_full = sem("aux_full")
            aux_act = sem("aux_act")
            aux_dve = sem("aux_dve")
            qk_done = sem("qk_done")
            max_done = sem("max_done")
            exp_done = sem("exp_done")
            pm_packed = sem("pm_packed")
            pt_done = sem("pt_done")
            pt_ev = sem("pt_ev")
            pv_done = sem("pv_done")
            rcp = sem("rcp")
            norm_done = sem("norm_done")
            t_top = sem("t_top")
            t_topi = sem("t_topi")
            t_topf = sem("t_topf")
            t_cand = sem("t_cand")
            t_best = sem("t_best")
            t_besti = sem("t_besti")
            t_rank = sem("t_rank")
            t_pick = sem("t_pick")
            t_prod = sem("t_prod")
            t_key = sem("t_key")
            t_high = sem("t_high")
            tab_ready = sem("tab_ready")

            USES = ([("zT0", "D"), ("zT1", "D")] + [(f"qk{m}", "A") for m in range(8)]
                    + [(f"v{m}", "A") for m in range(4)]
                    + [("tab0", "D"), ("pm0", "D"), ("sc0", "A"), ("pm1", "D"), ("sc1", "A"),
                       ("oT0", "A"), ("oT1", "A"), ("pm2", "D"), ("wo0", "D"), ("pm3", "D"),
                       ("tab1", "D"), ("sc2", "A"), ("sc3", "A"), ("oT2", "A"), ("oT3", "A"), ("wo1", "D")])
            NU = len(USES)
            UI = {name: n for n, (name, _) in enumerate(USES)}
            NA = sum(e == "A" for _, e in USES)
            ND = NU - NA
            assert NU % 2 == 0

            def emptied(name):
                u = UI[name]
                who = USES[u][1]
                return who, sum(e == who for _, e in USES[:u + 1])

            def wait_emptied(eng, i, name):
                who, n = emptied(name)
                eng.wait_ge(aux_act if who == "A" else aux_dve, i * (NA if who == "A" else ND) + n)

            def bank(name):
                return aux[UI[name] % 2]

            def split3(pe, outp, wh, wl, xh, xl, first, last):
                pe.matmul(outp, wl, xh, start=first, stop=False)
                pe.matmul(outp, wh, xl, start=False, stop=False)
                return pe.matmul(outp, wh, xh, start=False, stop=last)

            block = ctx.enter_context(nc.Block())

            @block.sync
            def _(sp):
                sp.dma_start(xin[:], x_blk[0]).then_inc(d_xin, 16)
                sp.dma_start(gam[:], gamma.rearrange("(k p) -> p k", p=P), allow_slow_non_contiguous=True).then_inc(d_small, 16)
                sp.dma_start(nrm[:], norm_w.rearrange("(k p) -> p k", p=P), allow_slow_non_contiguous=True).then_inc(d_small, 16)
                pmk_rows = pm_k.rearrange("(a h) p d -> (h p) a d", a=2)
                for copy in range(2):
                    sp.dma_start(pmk2[:, :, copy * DH:(copy + 1) * DH], pmk_rows).then_inc(d_small, 16)
                sp.dma_start(raw[:, 0:KD * 3 * INNER].rearrange("p (k n) -> p k n", k=KD),
                             w_qkv.rearrange("(k p) n -> p k n", p=P)).then_inc(d_raw, 16)
                sp.dma_start(raw[0:NK, KD * 3 * INNER:].rearrange("p (h n) -> p h n", h=EH),
                             keys.rearrange("h k s d -> k h (s d)")).then_inc(d_wq, 16)
                wq_rows = w_q.rearrange("(m p) d -> p m d", p=P)
                sp.dma_start(v[:].rearrange("p w (m d) -> p (w m) d", d=D), wq_rows[:, 0:8]).then_inc(d_wq, 16)
                sp.dma_start(sc[:].rearrange("p w (m d) -> p (w m) d", d=D), wq_rows[:, 8:16]).then_inc(d_wq, 16)
                sp.dma_start(wout[:], w_out.rearrange("(c p) n -> p c n", p=P)).then_inc(d_wout, 16)
                sp.wait_ge(c_pmv0, 1)
                for hh in range(8):
                    sp.dma_start(pmv_bd[hh * PM:(hh + 1) * PM, :, hh * DH:(hh + 1) * DH],
                                 pm_v.rearrange("(a h) p d -> h p a d", a=2)[hh]).then_inc(d_pmv, 16)

                def body(i, first, last):
                    wait_emptied(sp, i, "zT1")
                    sp.dma_start(z_scratch[i], zhl[:].rearrange("p a k t -> p (a k t)").bitcast(F32)).then_inc(st_z, 16)
                    if not last:
                        sp.wait_ge(z_ready, W * i + W)
                        sp.dma_start(xin[:], x_blk[i + 1]).then_inc(d_xin, 16)
                    if not first:
                        wait_emptied(sp, i - 1, "wo1")
                    sp.dma_start(xres[:], x_blk[i]).then_inc(d_xres, 16)
                    wait_emptied(sp, i, "tab0")
                    sp.dma_start(tab_scratch[W * i], tabT[:, 0].rearrange("p a q -> p (a q)")).then_inc(st_tab[0], 16)
                    wait_emptied(sp, i, "wo0")
                    sp.dma_start(out_blk[i, :, 0], y[:, 0]).then_inc(st_y[0], 16)
                    wait_emptied(sp, i, "tab1")
                    sp.dma_start(tab_scratch[W * i + 1], tabT[:, 1].rearrange("p a q -> p (a q)")).then_inc(st_tab[1], 16)
                    wait_emptied(sp, i, "wo1")
                    sp.dma_start(out_blk[i, :, 1], y[:, 1]).then_inc(st_y[1], 16)

                body(0, True, False)
                sp.wait_ge(w_split, KD)
                sp.wait_ge(set_ev, 3)
                sp.dma_start(upw[:], expert_up.rearrange("(p c) d -> p c d", c=LO)).then_inc(d_small, 16)
                with sp.Fori(1, NI - 1) as i:
                    body(i, False, False)
                body(NI - 1, False, True)
                for w in range(W):
                    sp.wait_ge(aux_dve, NI * ND + w + 1)
                    sp.dma_start(tab_scratch[W * NI + w], tabT[:, w].rearrange("p a q -> p (a q)")).then_inc(st_tab[w], 16)
                sp.wait_ge(st_z, 16 * NI)
                for w in range(W):
                    sp.wait_ge(st_tab[w], 16 * (NI + 1))
                    sp.wait_ge(st_y[w], 16 * NI)
                sp.wait_ge(d_small, 16 * 5)

            @block.gpsimd
            def _(pool):
                pool.memset(ident[:], 0.0).then_inc(c_ident, 1)
                pool.wait_ge(c_ident, 1)
                pool.affine_select(out=ident[:], in_=ident[:], compare_op=ALU.not_equal, fill=1.0, base=0,
                                   pattern=[[-1, P]], channel_multiplier=1).then_inc(c_ident, 1)
                pool.memset(minus_half[:], -0.5).then_inc(c_roots, 1)
                pool.memset(eps[:, 0], 1e-5).then_inc(c_roots, 1)
                pool.memset(eps[:, 1], 1e-6).then_inc(c_roots, 1)
                pool.memset(one[:], 1.0).then_inc(c_roots, 1)
                pool.memset(pmv_bd[:], 0.0).then_inc(c_pmv0, 1)
                for w in range(W):
                    pool.memset(tab[:, w], 0.0).then_inc(tab_ready, 1)
                pool.memset(identb[:], 0.0).then_inc(c_mask, 1)
                pool.memset(maskneg[:], 0.0).then_inc(c_mask, 1)
                pool.wait_ge(c_mask, 2)
                pool.affine_select(out=identb[:], in_=identb[:], compare_op=ALU.not_equal, fill=1.0, base=0,
                                   pattern=[[-1, P]], channel_multiplier=1).then_inc(c_mask, 1)
                pool.affine_select(out=maskneg[:, PM:KJ], in_=maskneg[:, PM:KJ], compare_op=ALU.is_ge, fill=-1e37,
                                   base=0, pattern=[[-1, SEG]], channel_multiplier=1).then_inc(c_mask, 1)
                pool.iota(iota8[:], pattern=[[1, TOP]], base=0, channel_multiplier=0,
                          allow_small_or_imprecise_dtypes=True).then_inc(c_iota, 1)

                def roots(i):
                    b = 6 * i
                    pool.wait_ge(ln_mv, W * i + W)
                    pool.tensor_tensor(out=rr[:, 0], in0=mv[:, :, 1], in1=eps[:, 0], op=ALU.add).then_inc(ln_step, 1)
                    pool.wait_ge(ln_step, b + 1)
                    pool.tensor_tensor(out=rr[:, 1], in0=rr[:, 0], in1=minus_half[:], op=ALU.pow).then_inc(ln_step, 1)
                    pool.wait_ge(ln_step, b + 2)
                    pool.tensor_tensor(out=rr[:, 2], in0=rr[:, 1], in1=rr[:, 1], op=ALU.mult).then_inc(ln_step, 1)
                    pool.wait_ge(ln_step, b + 3)
                    pool.tensor_tensor(out=rr[:, 3], in0=rr[:, 2], in1=mv[:, :, 1], op=ALU.mult).then_inc(ln_step, 1)
                    pool.wait_ge(ln_step, b + 4)
                    pool.tensor_tensor(out=rr[:, 2], in0=rr[:, 3], in1=eps[:, 1], op=ALU.add).then_inc(ln_step, 1)
                    pool.wait_ge(ln_step, b + 5)
                    pool.tensor_tensor(out=rr[:, 4], in0=rr[:, 2], in1=minus_half[:], op=ALU.pow).then_inc(ln_step, 1)
                    pool.wait_ge(ln_step, b + 6)
                    pool.tensor_tensor(out=rr[:, 5], in0=rr[:, 4], in1=rr[:, 1], op=ALU.mult).then_inc(ln_r, 1)

                def body(i, last):
                    for half in range(4):
                        if half == 2 and not last:
                            roots(i + 1)
                        pool.wait_ge(exp_done, NG * i + 2 * half + 2)
                        if half >= 2:
                            pool.wait_ge(aux_full, NU * i + UI[f"pm{half - 2}"] + 1)
                        pool.tensor_tensor(out=probpm[:, half % 2], in0=prob[half % 2][:, :, 0:PM],
                                           in1=one[:].unsqueeze(2).broadcast_to([P, 8, PM]),
                                           op=ALU.mult).then_inc(pm_packed, 1)

                pool.wait_ge(c_roots, 4)
                roots(0)
                body(0, False)
                with pool.Fori(1, NI - 1) as i:
                    body(i, False)
                body(NI - 1, True)

            @block.scalar
            def _(act):
                act.preload_act_table(ACT.Exp)

                def empty(i, name, outp, inp, scale=1.0):
                    act.wait_ge(aux_full, NU * i + UI[name] + 1)
                    act.activation(outp, inp, ACT.Copy, scale=scale).then_inc(aux_act, 1)

                def body(i, first):
                    for m in range(4):
                        empty(i, f"qk{m}", qT[:, 2 * m:2 * m + 2, :],
                              bank(f"qk{m}")[:].rearrange("p (c t) -> p c t", c=2), scale=ROOT)
                    for m in range(4):
                        empty(i, f"qk{4 + m}", kT[:, 2 * m:2 * m + 2, :, PM:KJ],
                              bank(f"qk{4 + m}")[:].rearrange("p (c w t) -> p c w t", c=2, w=W))
                    for m in range(4):
                        empty(i, f"v{m}", v[:, m // 2, (m % 2) * BANK:(m % 2 + 1) * BANK], bank(f"v{m}")[:])

                    def empty_sc(m):
                        if m % 2 == 0 and not first:
                            act.wait_ge(t_topi, W * i + m // 2 - 1)
                        empty(i, f"sc{m}", sc[:, m // 2, (m % 2) * BANK:(m % 2 + 1) * BANK], bank(f"sc{m}")[:])

                    def empty_oT(m):
                        empty(i, f"oT{m}", oT[:, 4 * (m % 2):4 * (m % 2) + 4, :],
                              bank(f"oT{m}")[:].rearrange("p (c t) -> p c t", c=4))

                    for n in range(NG):
                        act.wait_ge(max_done, NG * i + n + 1)
                        if n % 2 == 0 and (n >= 4 or not first):
                            act.wait_ge(pm_packed, 4 * i + n // 2 - 1)
                        for j in range(2):
                            for par in range(2):
                                slot = 4 * (n % 2) + 2 * j + par
                                last = act.activation(
                                    prob[n // 2 % 2][:, slot, :], sim[n % 2][:, par, j * KJ:(j + 1) * KJ], ACT.Exp,
                                    bias=negmax[:, n, par, j:j + 1], scale=1.0,
                                    accum_out=rowsum[:, n, 2 * j + par:2 * j + par + 1])
                        last.then_inc(exp_done, 1)
                        if n == 2:
                            empty_sc(0)
                        if n == 4:
                            empty_sc(1)
                        if n == 5:
                            empty_oT(0)
                            empty_oT(1)
                        act.wait_ge(pt_done, NG * i + n + 1)
                        act.activation(probT[n % 2][:], ptb[:], ACT.Copy).then_inc(pt_ev, 1)
                    empty_sc(2)
                    empty_sc(3)
                    empty_oT(2)
                    empty_oT(3)

                body(0, True)
                with act.Fori(1, NI) as i:
                    body(i, False)

            @block.vector
            def _(dve):
                dve.wait_ge(d_small, 16 * 4)
                dve.wait_ge(d_raw, 16)
                for k in range(KD):
                    rw = raw[:, k * 3 * INNER:(k + 1) * 3 * INNER]
                    dve.tensor_scalar(out=wqkv_h[:, k], in0=rw, scalar1=gam[:, k:k + 1], scalar2=None,
                                      op0=ALU.mult).then_inc(w_hi, 1)
                    dve.wait_ge(w_hi, k + 1)
                    dve.scalar_tensor_tensor(out=wqkv_l[:, k], in0=rw, scalar=gam[:, k:k + 1],
                                             in1=wqkv_h[:, k].bitcast(F32), op0=ALU.mult,
                                             op1=ALU.subtract).then_inc(w_split, 1)
                dve.wait_ge(set_ps, 1)
                for half in range(2):
                    rows = aux[0][:, half * P:(half + 1) * P].rearrange("p (c e s) -> p c e s", e=2, s=PM)
                    for par in range(2):
                        for w in range(W):
                            last = dve.tensor_copy(kT[par * DH:(par + 1) * DH, 4 * half:4 * half + 4, w, 0:PM],
                                                   rows[par * DH:(par + 1) * DH, :, par, :])
                last.then_inc(set_ev, 1)
                for n in range(2):
                    dve.wait_ge(set_ps, 2 + n)
                    dve.tensor_copy(o[:, n * BANK:(n + 1) * BANK], aux[(1 + n) % 2][:]).then_inc(set_ev, 1)
                for k in range(KD):
                    for n in range(2):
                        u = 3 + 2 * k + n
                        dve.wait_ge(set_ps, u + 1)
                        hi = wsc_h[:, k, n * BANK:(n + 1) * BANK]
                        dve.tensor_scalar(out=hi, in0=aux[u % 2][:], scalar1=nrm[:, k:k + 1], scalar2=None,
                                          op0=ALU.mult).then_inc(w_hi, 1)
                        dve.wait_ge(w_hi, KD + 2 * k + n + 1)
                        dve.scalar_tensor_tensor(out=wsc_l[:, k, n * BANK:(n + 1) * BANK], in0=aux[u % 2][:],
                                                 scalar=nrm[:, k:k + 1], in1=hi.bitcast(F32), op0=ALU.mult,
                                                 op1=ALU.subtract).then_inc(set_ev, 1)

                def moments(i):
                    dve.wait_ge(d_xin, 16 * i + 16)
                    for w in range(W):
                        dve.bn_stats(stats[:, w], xin[:, w]).then_inc(ln_bn, 1)

                def aggregate():
                    for w in range(W):
                        dve.bn_aggr(mv[:, w], stats[:, w]).then_inc(ln_mv, 1)

                def normed(i, first=False):
                    dve.wait_ge(ln_r, i + 1)
                    dve.wait_ge(ln_mv, W * i + W)
                    for w in range(W):
                        dve.tensor_scalar(out=z[:, w], in0=xin[:, w], scalar1=mv[:, w, 0:1],
                                          scalar2=rr[:, 5, w:w + 1], op0=ALU.subtract,
                                          op1=ALU.mult).then_inc(z_ready, 1)

                def split_z(i, first):
                    if not first:
                        dve.wait_ge(st_z, 16 * i)
                    for w in range(W):
                        dve.wait_ge(aux_full, NU * i + w + 1)
                        src = bank(f"zT{w}")[:, 0:KD * P].rearrange("p (k t) -> p k t", k=KD)
                        hi = zhl[:, 0, :, w * P:(w + 1) * P]
                        dve.tensor_copy(hi, src).then_inc(z_hi, 1)
                        dve.wait_ge(z_hi, W * i + w + 1)
                        dve.tensor_tensor(out=zhl[:, 1, :, w * P:(w + 1) * P], in0=src, in1=hi.bitcast(F32),
                                          op=ALU.subtract).then_inc(aux_dve, 1)

                def choose(t, w):
                    s3 = sc[:, w].rearrange("p (m k) -> p m k", k=NK)

                    def tops(m0):
                        for m in range(m0, m0 + 8):
                            last = dve.max(top[:, m], s3[:, m])
                        if m0 == 8:
                            last.then_inc(t_top, 1)

                    def pairs():
                        dve.wait_ge(t_top, t + 1)
                        a = top[:].rearrange("p (h s) k -> p h s k", s=2)
                        dve.tensor_tensor(
                            out=cand[:], in0=a[:, :, 0, :].unsqueeze(3).broadcast_to([P, EH, TOP, TOP]),
                            in1=a[:, :, 1, :].unsqueeze(2).broadcast_to([P, EH, TOP, TOP]),
                            op=ALU.add).then_inc(t_cand, 1)

                    def topis(m0):
                        for m in range(m0, m0 + 8):
                            last = dve.max_index(topi[:, m], top[:, m], s3[:, m])
                        if m0 == 8:
                            last.then_inc(t_topi, 1)

                    def bests():
                        dve.wait_ge(t_topi, t + 1)
                        dve.wait_ge(t_cand, t + 1)
                        dve.tensor_copy(topf[:], topi[:]).then_inc(t_topf, 1)
                        for h in range(EH):
                            last = dve.max(best[:, h * TOP:(h + 1) * TOP], cand[:, h].rearrange("p a b -> p (a b)"))
                        last.then_inc(t_best, 1)

                    def twice(a):
                        return a.unsqueeze(1).broadcast_to([P, 2, NC])

                    def bestis():
                        dve.wait_ge(t_best, t + 1)
                        dve.tensor_scalar(out=tab[:, w, 2], in0=twice(best[:]), scalar1=0.0, scalar2=None,
                                          op0=ALU.max)
                        for h in range(EH):
                            last = dve.max_index(besti[:, h * TOP:(h + 1) * TOP], best[:, h * TOP:(h + 1) * TOP],
                                                 cand[:, h].rearrange("p a b -> p (a b)"))
                        last.then_inc(t_besti, 1)

                    def ranks():
                        dve.wait_ge(t_besti, t + 1)
                        dve.tensor_scalar(out=rank[:, 0], in0=besti[:], scalar1=3, scalar2=None,
                                          op0=ALU.logical_shift_right)
                        dve.tensor_scalar(out=rank[:, 1], in0=besti[:], scalar1=7, scalar2=None,
                                          op0=ALU.bitwise_and).then_inc(t_rank, 1)

                    def lookup(s):
                        if s == 1:
                            dve.wait_ge(t_key, 2 * t + 1)
                        if s == 0:
                            dve.wait_ge(t_rank, t + 1)
                            dve.wait_ge(t_topf, t + 1)
                        dve.tensor_tensor(out=pick[:], in0=rank[:, s].unsqueeze(2).broadcast_to([P, NC, TOP]),
                                          in1=iota8[:].unsqueeze(1).broadcast_to([P, NC, TOP]),
                                          op=ALU.is_equal).then_inc(t_pick, 1)
                        dve.wait_ge(t_pick, 2 * t + s + 1)
                        f = topf[:].rearrange("p (h s) k -> p h s k", s=2)[:, :, s, :]
                        dve.tensor_tensor(
                            out=prod[:].rearrange("p (h c) a -> p h c a", c=TOP),
                            in0=pick[:].rearrange("p (h c) a -> p h c a", c=TOP),
                            in1=f.unsqueeze(2).broadcast_to([P, EH, TOP, TOP]), op=ALU.mult).then_inc(t_prod, 1)
                        dve.wait_ge(t_prod, 2 * t + s + 1)
                        dve.tensor_reduce(out=keyi[:, s], in_=prod[:], axis=AX.X, op=ALU.add).then_inc(t_key, 1)

                    def table():
                        dve.wait_ge(t_key, 2 * t + 2)
                        dve.tensor_scalar(out=high[:], in0=keyi[:, 1], scalar1=float(LO), scalar2=None,
                                          op0=ALU.is_ge).then_inc(t_high, 1)
                        dve.wait_ge(t_high, t + 1)
                        dve.scalar_tensor_tensor(out=tab[:, w, 0], in0=twice(keyi[:, 0]), scalar=float(NK // LO),
                                                 in1=twice(high[:]), op0=ALU.mult, op1=ALU.add)
                        dve.scalar_tensor_tensor(out=tab[:, w, 1], in0=twice(high[:]), scalar=-float(LO),
                                                 in1=twice(keyi[:, 1]), op0=ALU.mult,
                                                 op1=ALU.add).then_inc(tab_ready, 1)

                    return [lambda: tops(0), lambda: tops(8), pairs, lambda: topis(0), lambda: topis(8), bests,
                            bestis, ranks, lambda: lookup(0), lambda: lookup(1), table]

                def empty_tab(i, w, first):
                    if not first:
                        dve.wait_ge(st_tab[w], 16 * i)
                    dve.wait_ge(aux_full, NU * i + UI[f"tab{w}"] + 1)
                    src = bank(f"tab{w}")[:, 0:3 * P].rearrange("p (a t) -> p a t", a=3)
                    dve.tensor_copy(tabT[0:64, w], src[0:64, :, 0:64])
                    dve.tensor_copy(tabT[64:128, w], src[64:128, :, 64:128]).then_inc(aux_dve, 1)

                def body(i, first, last):
                    if not first:
                        wait_emptied(dve, i - 1, "sc3")
                        dve.wait_ge(tab_ready, W * i)
                    split_z(i, first)
                    later = []
                    if not first:
                        for piece in choose(W * i - W, 0):
                            piece()
                        later = choose(W * i - W + 1, 1)

                    def maxima(n):
                        dve.wait_ge(qk_done, NG * i + n + 1)
                        dve.tensor_reduce(out=negmax[:, n], in_=sim[n % 2][:, :, 0:2 * KJ].rearrange(
                            "p e (j k) -> p e j k", k=KJ), axis=AX.X, op=ALU.max, negate=True).then_inc(max_done, 1)

                    def empty_pm(half):
                        dve.wait_ge(aux_full, NU * i + UI[f"pm{half}"] + 1)
                        dve.tensor_copy(pmT[:, half % 2], bank(f"pm{half}")[:, 0:P]).then_inc(aux_dve, 1)

                    def normalise(half):
                        dve.wait_ge(exp_done, NG * i + 2 * half + 2)
                        if half > 0 or not first:
                            dve.wait_ge(norm_done, 4 * i + half)
                        dve.reciprocal(recip[:], rowsum[:, 2 * half:2 * half + 2].rearrange("p a b -> p (a b)")
                                       ).then_inc(rcp, 1)
                        dve.wait_ge(rcp, 4 * i + half + 1)
                        dve.wait_ge(pv_done, 4 * i + half + 1)
                        dve.tensor_tensor(
                            out=o[:, (half % 2) * BANK:(half % 2 + 1) * BANK].rearrange("p (h d) -> p h d", d=DH),
                            in0=pvb[:].rearrange("p (h d) -> p h d", d=DH),
                            in1=recip[:].unsqueeze(2).broadcast_to([P, 8, DH]), op=ALU.mult).then_inc(norm_done, 1)

                    def add_x(w):
                        if w == 0:
                            dve.wait_ge(d_xres, 16 * i + 16)
                        if not first:
                            dve.wait_ge(st_y[w], 16 * i)
                        dve.wait_ge(aux_full, NU * i + UI[f"wo{w}"] + 1)
                        dve.tensor_tensor(out=y[:, w], in0=bank(f"wo{w}")[:, 0:D], in1=xres[:, w],
                                          op=ALU.add).then_inc(aux_dve, 1)

                    maxima(0)
                    for n in range(NG):
                        if n == 3 and not last:
                            dve.wait_ge(ln_bn, W * i + 2 * W)
                        if n == 0 and later:
                            dve.wait_ge(tab_ready, W * i + 1)
                        if n + 1 < NG:
                            maxima(n + 1)
                        if n == 3 and not last:
                            aggregate()
                        if n == 1:
                            empty_tab(i, 0, first)
                        if n == 6:
                            add_x(0)
                        if n % 2 == 1:
                            empty_pm(n // 2)
                        if n >= 2 and n % 2 == 0:
                            normalise(n // 2 - 1)
                        if n == 2 and not last:
                            moments(i + 1)
                        if n == 5 and not last:
                            normed(i + 1)
                        for piece in later[2 * n:2 * n + 2]:
                            piece()
                    normalise(3)
                    empty_tab(i, 1, first)
                    add_x(1)

                moments(0)
                dve.wait_ge(ln_bn, W)
                aggregate()
                normed(0)
                dve.wait_ge(c_iota, 1)
                body(0, True, False)
                with dve.Fori(1, NI - 1) as i:
                    body(i, False, False)
                body(NI - 1, False, True)
                for w in range(W):
                    wait_emptied(dve, NI - 1, f"sc{2 * w + 1}")
                    dve.wait_ge(tab_ready, W * NI + w)
                    for piece in choose(W * (NI - 1) + w, w):
                        piece()
                for w in range(W):
                    dve.wait_ge(st_tab[w], 16 * NI)
                    dve.wait_ge(aux_full, NU * NI + w + 1)
                    src = aux[w][:, 0:3 * P].rearrange("p (a t) -> p a t", a=3)
                    dve.tensor_copy(tabT[0:64, w], src[0:64, :, 0:64])
                    dve.tensor_copy(tabT[64:128, w], src[64:128, :, 64:128]).then_inc(aux_dve, 1)

            @block.tensor
            def _(pe):
                pe.wait_ge(c_ident, 2)
                pe.wait_ge(d_small, 16 * 4)
                for half in range(2):
                    last = pe.transpose(aux[0][:, half * P:(half + 1) * P], pmk2[:, half], ident[:])
                last.then_inc(set_ps, 1)
                pe.wait_ge(d_wq, 16 * 3)
                keyrows = raw[0:NK, KD * 3 * INNER:].rearrange("p (m d) -> p m d", d=DK)
                for n in range(2):
                    if n == 1:
                        pe.wait_ge(set_ev, 1)
                    for m in range(8):
                        last = pe.transpose(aux[(1 + n) % 2][:, m * NK:(m + 1) * NK], keyrows[:, 8 * n + m],
                                            ident[0:NK, 0:NK])
                    last.then_inc(set_ps, 1)
                for k in range(KD):
                    for n in range(2):
                        u = 3 + 2 * k + n
                        pe.wait_ge(set_ev, 3 if u == 3 else u - 1)
                        rows = (v if n == 0 else sc)[:].rearrange("p w (m d) -> p (w m) d", d=D)
                        for m in range(8):
                            last = pe.matmul(aux[u % 2][:, m * NK:(m + 1) * NK], rows[:, m, k * P:(k + 1) * P],
                                             o[:, (8 * n + m) * NK:(8 * n + m + 1) * NK], start=True, stop=True)
                        last.then_inc(set_ps, 1)
                pe.wait_ge(set_ev, 7)
                pe.wait_ge(w_split, KD)
                pe.wait_ge(c_mask, 4)

                def use(i, name, first):
                    u = UI[name]
                    if u >= 2:
                        wait_emptied(pe, i, USES[u - 2][0])
                    elif not first:
                        wait_emptied(pe, i - 1, USES[u - 2][0])
                    return bank(name)

                def body(i, first):
                    pe.wait_ge(z_ready, W * i + W)
                    for w in range(W):
                        b = use(i, f"zT{w}", first)
                        for k in range(KD):
                            last = pe.transpose(b[:, k * P:(k + 1) * P], z[:, w, k * P:(k + 1) * P], ident[:])
                        last.then_inc(aux_full, 1)
                    wait_emptied(pe, i, "zT1")
                    for m in range(8):
                        b = use(i, f"qk{m}", first)
                        for c in range(2):
                            cols = slice((2 * m + c) * P, (2 * m + c + 1) * P)
                            for k in range(KD):
                                last = split3(pe, b[:, c * BLK:(c + 1) * BLK], wqkv_h[:, k, cols], wqkv_l[:, k, cols],
                                              zhl[:, 0, k], zhl[:, 1, k], k == 0, k == KD - 1)
                        last.then_inc(aux_full, 1)

                    def rows_times(name, wh, wl, w, n0):
                        b = use(i, name, first)
                        tok = slice(w * P, (w + 1) * P)
                        for k in range(KD):
                            last = split3(pe, b[:], zhl[:, 0, k, tok], zhl[:, 1, k, tok], wh[:, k, n0:n0 + BANK],
                                          wl[:, k, n0:n0 + BANK], k == 0, k == KD - 1)
                        last.then_inc(aux_full, 1)

                    for m in range(4):
                        rows_times(f"v{m}", wqkv_h, wqkv_l, m // 2, 2 * INNER + (m % 2) * BANK)

                    def scores(m):
                        rows_times(f"sc{m}", wsc_h, wsc_l, m // 2, (m % 2) * BANK)

                    def qk(n):
                        w = n // 4
                        if n >= 2:
                            pe.wait_ge(exp_done, NG * i + n - 1)
                        elif not first:
                            pe.wait_ge(exp_done, NG * i + n - 1)
                        if n == 0:
                            wait_emptied(pe, i, "qk7")
                        for par in range(2):
                            pe.matmul(sim[n % 2][:, par, 0:2 * KJ].rearrange("p (j k) -> p j k", k=KJ), identb[:],
                                      maskneg[:].unsqueeze(1).broadcast_to([P, 2, KJ]), start=True, stop=False)
                        for j in range(2):
                            for par in range(2):
                                c = 2 * (n % 4) + j
                                rows = slice(par * DH, (par + 1) * DH)
                                last = pe.matmul(sim[n % 2][:, par, j * KJ:(j + 1) * KJ],
                                                 qT[rows, c, w * P:(w + 1) * P], kT[rows, c, w, :],
                                                 start=False, stop=(j == 1))
                        last.then_inc(qk_done, 1)

                    def transpose_probs(n):
                        pe.wait_ge(exp_done, NG * i + n + 1)
                        if n >= 1 or not first:
                            pe.wait_ge(pt_ev, NG * i + n)
                        for hh in range(4):
                            last = pe.transpose(ptb[:, hh], prob[n // 2 % 2][:, 4 * (n % 2) + hh, PM:KJ], ident[:])
                        last.then_inc(pt_done, 1)

                    def transpose_pm(half):
                        b = use(i, f"pm{half}", first)
                        pe.wait_ge(pm_packed, 4 * i + half + 1)
                        pe.transpose(b[:, 0:P], probpm[:, half % 2].rearrange("p h s -> p (h s)"),
                                     ident[:]).then_inc(aux_full, 1)

                    def pv(n):
                        half = n // 2
                        if n == 0:
                            wait_emptied(pe, i, "v3")
                        if n % 2 == 0 and (half > 0 or not first):
                            pe.wait_ge(norm_done, 4 * i + half)
                        pe.wait_ge(pt_ev, NG * i + n + 1)
                        for hh in range(4):
                            head = 4 * (n % 4) + hh
                            slot = 4 * (n % 2) + hh
                            pe.matmul(pvb[:, slot * DH:(slot + 1) * DH], probT[n % 2][:, hh],
                                      v[:, n // 4, head * DH:(head + 1) * DH], start=(slot == 0), stop=False)
                        if n % 2 == 1:
                            wait_emptied(pe, i, f"pm{half}")
                            pe.matmul(pvb[:], pmT[:, half % 2], pmv_bd[:, half % 2], start=False,
                                      stop=True).then_inc(pv_done, 1)

                    def transpose_o(m):
                        b = use(i, f"oT{m}", first)
                        pe.wait_ge(norm_done, 4 * i + m + 1)
                        for c in range(4):
                            cc = 4 * (m % 2) + c
                            last = pe.transpose(b[:, c * P:(c + 1) * P], o[:, cc * P:(cc + 1) * P], ident[:])
                        last.then_inc(aux_full, 1)

                    def project(w):
                        b = use(i, f"wo{w}", first)
                        wait_emptied(pe, i, f"oT{2 * w + 1}")
                        for c in range(CH):
                            last = pe.matmul(b[:, 0:D], oT[:, c], wout[:, c], start=(c == 0), stop=(c == CH - 1))
                        last.then_inc(aux_full, 1)

                    def transpose_tab(w):
                        b = use(i, f"tab{w}", first)
                        pe.wait_ge(tab_ready, W * i + w + 1)
                        for a in range(3):
                            last = pe.transpose(b[:, a * P:(a + 1) * P], tab[:, w, a].rearrange("p e c -> p (e c)"),
                                                ident[:])
                        last.then_inc(aux_full, 1)

                    qk(0)
                    for n in range(NG):
                        if n + 1 < NG:
                            qk(n + 1)
                        if n == 1:
                            transpose_tab(0)
                        if n == 2:
                            scores(0)
                        if n == 4:
                            scores(1)
                        if n == 5:
                            transpose_o(0)
                            transpose_o(1)
                        if n == 6:
                            project(0)
                        transpose_probs(n)
                        if n % 2 == 1:
                            transpose_pm(n // 2)
                        if n >= 1:
                            pv(n - 1)
                    pv(7)
                    transpose_tab(1)
                    scores(2)
                    scores(3)
                    transpose_o(2)
                    transpose_o(3)
                    project(1)

                pe.wait_ge(d_wout, 16)
                pe.wait_ge(d_pmv, 16 * 8)
                body(0, True)
                with pe.Fori(1, NI) as i:
                    body(i, False)
                for w in range(W):
                    wait_emptied(pe, NI - 1, USES[NU - 2 + w][0])
                    pe.wait_ge(tab_ready, W * NI + w + 1)
                    for a in range(3):
                        last = pe.transpose(aux[w][:, a * P:(a + 1) * P], tab[:, w, a].rearrange("p e c -> p (e c)"),
                                            ident[:])
                    last.then_inc(aux_full, 1)

        with ExitStack() as ctx:
            def sb(name, shape, dt):
                return ctx.enter_context(nc.sbuf_tensor(name, shape, dt))

            def ps(name, shape, dt=F32):
                return ctx.enter_context(nc.psum_tensor(name, shape, dt))

            UQ = 32
            NUN = BLK // 2 // UQ
            PC = 8
            NP = BLK // 2 // PC
            ND2 = LO // 2

            wd_h = sb("wd_h", [P, LO, KD, P], F32R)
            wd_l = sb("wd_l", [P, LO, KD, P], F32R)
            g = sb("g", [P, LO, BLK], F32)
            iota = sb("iota", [P, P, UQ], BF16)
            hmask = sb("hmask", [P, 2], F32)
            left = [sb(f"left{n}", [P, P, UQ], BF16) for n in range(2)]
            onehot = sb("onehot", [P, LO, UQ], BF16)
            right = [sb(f"right{n}", [P, 3, LO, 2, UQ], BF16) for n in range(2)]
            tb = sb("tb", [P, W, 3, NC], F32)
            ids = sb("ids", [P, 2, W, NC], BF16)
            part = sb("part", [P, 3, W, NC], BF16)
            rest = sb("rest", [P, W, NC], F32)
            wpart = sb("wpart", [P, 3, 2, W, NC], BF16)
            zb = sb("zb", [P, 2, KD, BLK], F32R)
            yb = sb("yb", [P, W, D], F32)
            res = sb("res", [P, W, D], F32)

            dps = [ps(f"dps{n}", [P, 2, BLK]) for n in range(2)]
            cps = [ps(f"cps{n}", [P, PC, LO, 2]) for n in range(3)]
            ups = [ps(f"ups{n}", [P, BANK]) for n in range(2)]

            d_down = sem("d_down")
            c_iotab = sem("c_iotab")
            dt_ps = sem("dt_ps")
            dt_hi = sem("dt_hi")
            dt_ev = sem("dt_ev")
            d_zb = sem("d_zb")
            d_tb = sem("d_tb")
            d_yb = sem("d_yb")
            st_out = [sem(f"st_out{w}") for w in range(W)]
            p_ids = sem("p_ids")
            p_step = sem("p_step")
            p_w = sem("p_w")
            u_left = sem("u_left")
            u_one = sem("u_one")
            u_ready = sem("u_ready")
            down_done = sem("down_done")
            gelu_done = sem("gelu_done")
            c_done = sem("c_done")
            mul_done = sem("mul_done")
            up_done = sem("up_done")
            add_done = sem("add_done")

            block = ctx.enter_context(nc.Block())

            @block.sync
            def _(sp):
                sp.dma_start(g[:], expert_down.rearrange("(p c) d -> p c d", c=LO)).then_inc(d_down, 16)

                def body(i, first):
                    if not first:
                        sp.wait_ge(p_w, i)
                    for w in range(W):
                        sp.dma_start(tb[:, w].rearrange("p a q -> p (a q)"),
                                     tab_scratch[W * i + W + w]).then_inc(d_tb, 16)
                    if not first:
                        sp.wait_ge(down_done, ND2 * i)
                    sp.dma_start(zb[:].rearrange("p a k t -> p (a k t)").bitcast(F32), z_scratch[i]).then_inc(d_zb, 16)
                    if not first:
                        sp.wait_ge(add_done, W * i)
                        for w in range(W):
                            sp.dma_start(out_blk[i - 1, :, w], res[:, w]).then_inc(st_out[w], 16)
                    sp.dma_start(yb[:], out_blk[i]).then_inc(d_yb, 16)

                body(0, True)
                with sp.Fori(1, NI) as i:
                    body(i, False)
                sp.wait_ge(add_done, W * NI)
                for w in range(W):
                    sp.dma_start(out_blk[NI - 1, :, w], res[:, w]).then_inc(st_out[w], 16)
                for w in range(W):
                    sp.wait_ge(st_out[w], 16 * NI)

            @block.gpsimd
            def _(pool):
                pool.iota(iota[:], pattern=[[1, P], [0, UQ]], base=0, channel_multiplier=0,
                          allow_small_or_imprecise_dtypes=True).then_inc(c_iotab, 1)
                pool.memset(hmask[:], 1.0).then_inc(c_iotab, 1)
                pool.wait_ge(c_iotab, 2)
                pool.affine_select(out=hmask[:, 0:1], in_=hmask[:, 0:1], compare_op=ALU.is_ge, fill=0.0, base=63,
                                   pattern=[[0, 1]], channel_multiplier=-1).then_inc(c_iotab, 1)
                pool.affine_select(out=hmask[:, 1:2], in_=hmask[:, 1:2], compare_op=ALU.is_ge, fill=0.0, base=-64,
                                   pattern=[[0, 1]], channel_multiplier=1).then_inc(c_iotab, 1)

            @block.scalar
            def _(act):
                act.preload_act_table(ACT.Gelu)

                def body(i):
                    for m in range(ND2):
                        act.wait_ge(down_done, ND2 * i + m + 1)
                        act.activation(g[:, 2 * m:2 * m + 2], dps[m % 2][:], ACT.Gelu).then_inc(gelu_done, 1)

                body(0)
                with act.Fori(1, NI) as i:
                    body(i)

            @block.vector
            def _(dve):
                for u in range(LO * KD // 4):
                    k = u % KD
                    c0 = 4 * (u // KD)
                    src = dps[u % 2][:].rearrange("p a t -> p (a t)").rearrange("p (c e) -> p c e", c=4)
                    dve.wait_ge(dt_ps, u + 1)
                    dve.tensor_scalar(out=wd_h[:, c0:c0 + 4, k], in0=src, scalar1=nrm[:, k:k + 1], scalar2=None,
                                      op0=ALU.mult).then_inc(dt_hi, 1)
                    dve.wait_ge(dt_hi, u + 1)
                    dve.scalar_tensor_tensor(out=wd_l[:, c0:c0 + 4, k], in0=src, scalar=nrm[:, k:k + 1],
                                             in1=wd_h[:, c0:c0 + 4, k].bitcast(F32), op0=ALU.mult,
                                             op1=ALU.subtract).then_inc(dt_ev, 1)
                dve.wait_ge(c_iotab, 4)

                def prepare(i, first):
                    b = 4 * i
                    dve.wait_ge(d_tb, 16 * W * i + 16 * W)
                    if not first:
                        dve.wait_ge(u_ready, NUN * i)
                    for a in range(2):
                        last = dve.tensor_copy(ids[:, a], tb[:, :, a])
                    last.then_inc(p_ids, 1)
                    wt = tb[:, :, 2]
                    dve.tensor_copy(part[:, 0], wt).then_inc(p_step, 1)
                    dve.wait_ge(p_step, b + 1)
                    dve.tensor_tensor(out=rest[:], in0=wt, in1=part[:, 0], op=ALU.subtract).then_inc(p_step, 1)
                    dve.wait_ge(p_step, b + 2)
                    dve.tensor_copy(part[:, 1], rest[:]).then_inc(p_step, 1)
                    dve.wait_ge(p_step, b + 3)
                    dve.tensor_tensor(out=part[:, 2], in0=rest[:], in1=part[:, 1], op=ALU.subtract).then_inc(p_step, 1)
                    dve.wait_ge(p_step, b + 4)
                    for half in range(2):
                        last = dve.tensor_scalar(out=wpart[:, :, half], in0=part[:], scalar1=hmask[:, half:half + 1],
                                                 scalar2=None, op0=ALU.mult)
                    last.then_inc(p_w, 1)

                def build(i, u, first):
                    w, q0 = u // 2, (u % 2) * UQ
                    if u >= 2 or not first:
                        dve.wait_ge(c_done, NP * i + 4 * u - 4)
                    if u > 0:
                        dve.wait_ge(u_ready, NUN * i + u)
                    if u == 0:
                        dve.wait_ge(p_ids, i + 1)
                        dve.wait_ge(p_w, i + 1)
                    dve.tensor_tensor(out=left[u % 2][:],
                                      in0=ids[:, 0, w, q0:q0 + UQ].unsqueeze(1).broadcast_to([P, P, UQ]),
                                      in1=iota[:], op=ALU.is_equal)
                    dve.tensor_tensor(out=onehot[:],
                                      in0=ids[:, 1, w, q0:q0 + UQ].unsqueeze(1).broadcast_to([P, LO, UQ]),
                                      in1=iota[:, 0:LO], op=ALU.is_equal).then_inc(u_one, 1)
                    dve.wait_ge(u_one, NUN * i + u + 1)
                    for s in range(3):
                        last = dve.tensor_tensor(
                            out=right[u % 2][:, s], in0=onehot[:].unsqueeze(2).broadcast_to([P, LO, 2, UQ]),
                            in1=wpart[:, s, :, w, q0:q0 + UQ].unsqueeze(1).broadcast_to([P, LO, 2, UQ]), op=ALU.mult)
                    last.then_inc(u_ready, 1)

                def times_c(i, n):
                    w, q0 = n // 8, (n % 8) * PC
                    if n == 0:
                        dve.wait_ge(gelu_done, ND2 * i + ND2)
                    dve.wait_ge(c_done, NP * i + n + 1)
                    tok = g[:, :, w * P:(w + 1) * P].rearrange("p c (e q) -> p c e q", e=2)
                    for half in range(2):
                        gv = tok[:, :, half, q0:q0 + PC]
                        last = dve.tensor_tensor(out=gv, in0=cps[n % 3][:, :, :, half].rearrange("p q c -> p c q"),
                                                 in1=gv, op=ALU.mult)
                    last.then_inc(mul_done, 1)

                def finish(i, w, first):
                    if w == 0:
                        dve.wait_ge(d_yb, 16 * i + 16)
                    if not first:
                        dve.wait_ge(st_out[w], 16 * i)
                    dve.wait_ge(up_done, W * i + w + 1)
                    dve.tensor_tensor(out=res[:, w], in0=ups[w][:, 0:D], in1=yb[:, w], op=ALU.add).then_inc(add_done, 1)

                def body(i, first):
                    prepare(i, first)
                    build(i, 0, first)
                    build(i, 1, first)
                    for n in range(8):
                        times_c(i, n)
                    build(i, 2, first)
                    build(i, 3, first)
                    for n in range(8, 16):
                        times_c(i, n)
                    finish(i, 0, first)
                    finish(i, 1, first)

                body(0, True)
                with dve.Fori(1, NI) as i:
                    body(i, False)

            @block.tensor
            def _(pe):
                pe.wait_ge(d_down, 16)
                for u in range(LO * KD // 4):
                    k = u % KD
                    c0 = 4 * (u // KD)
                    dst = dps[u % 2][:].rearrange("p a t -> p (a t)")
                    if u >= 2:
                        pe.wait_ge(dt_ev, u - 1)
                    for c in range(4):
                        last = pe.transpose(dst[:, c * P:(c + 1) * P], g[:, c0 + c, k * P:(k + 1) * P], ident[:])
                    last.then_inc(dt_ps, 1)
                pe.wait_ge(dt_ev, LO * KD // 4)

                def body(i, first):
                    pe.wait_ge(d_zb, 16 * i + 16)
                    for m in range(ND2):
                        if m >= 2 or not first:
                            pe.wait_ge(gelu_done, ND2 * i + m - 1)
                        for c in range(2):
                            for k in range(KD):
                                last = split3(pe, dps[m % 2][:, c], wd_h[:, 2 * m + c, k], wd_l[:, 2 * m + c, k],
                                              zb[:, 0, k], zb[:, 1, k], k == 0, k == KD - 1)
                        last.then_inc(down_done, 1)

                    def c_pieces(u):
                        pe.wait_ge(u_ready, NUN * i + u + 1)
                        for pc in range(4):
                            n = 4 * u + pc
                            if n >= 3 or not first:
                                pe.wait_ge(mul_done, NP * i + n - 2)
                            for q in range(PC):
                                for s in range(3):
                                    last = pe.matmul(cps[n % 3][:, q], left[u % 2][:, :, pc * PC + q],
                                                     right[u % 2][:, s, :, :, pc * PC + q],
                                                     start=(s == 0), stop=(s == 2))
                            last.then_inc(c_done, 1)

                    def up(w):
                        pe.wait_ge(mul_done, NP * i + 8 * w + 8)
                        if not first:
                            pe.wait_ge(add_done, W * i - W + w + 1)
                        for c in range(LO):
                            last = pe.matmul(ups[w][:, 0:D], g[:, c, w * P:(w + 1) * P], upw[:, c],
                                             start=(c == 0), stop=(c == LO - 1))
                        last.then_inc(up_done, 1)

                    c_pieces(0)
                    c_pieces(1)
                    up(0)
                    c_pieces(2)
                    c_pieces(3)
                    up(1)

                body(0, True)
                with pe.Fori(1, NI) as i:
                    body(i, False)


_INS = ['L0_attn_x', 'L0_attn_gamma', 'L0_attn_w_qkv', 'L0_attn_w_out', 'L0_attn_pm_k', 'L0_attn_pm_v',
        'L0_ffn_w_q', 'L0_ffn_keys', 'L0_ffn_expert_down', 'L0_ffn_expert_up', 'L0_ffn_norm_w']


def kernel(**inputs):
    import numpy as np
    import concourse.bacc as bacc
    from concourse.bass_utils import run_bass_kernel_spmd

    nc = bacc.Bacc("TRN2", target_bir_lowering=False, num_devices=1)
    arrays, args = {}, []
    for name in _INS:
        a = np.ascontiguousarray(inputs[name])
        arrays[f"in_{name}"] = a
        args.append(nc.dram_tensor(f"in_{name}", a.shape, mybir.dt.from_np(a.dtype), kind="ExternalInput").ap())
    shape = arrays['in_L0_attn_x'].shape
    args.append(nc.dram_tensor("out_0", shape, F32, kind="ExternalOutput").ap())
    attention_experts(nc, *args)
    r = run_bass_kernel_spmd(nc, [arrays], core_ids=[0])
    return r.results[0]["out_0"]
```

```python
from contextlib import ExitStack

import concourse.bass as bass
from concourse import mybir

ALU = mybir.AluOpType
ACT = mybir.ActivationFunctionType
AX = mybir.AxisListType
F32 = mybir.dt.float32
F32R = mybir.dt.float32r
BF16 = mybir.dt.bfloat16
F16 = mybir.dt.float16
U32 = mybir.dt.uint32

P = 128
BANK = 512
SEG = 128
W = 2
BLK = W * SEG
TOP = 8


def attention_experts(nc, x, gamma, w_qkv, w_out, pm_k, pm_v, w_q, keys, expert_down, expert_up, norm_w, out):
    B, S, D = x.shape
    HEADS, PM, DH = pm_k.shape
    EH, NK, _, DK = keys.shape
    INNER = HEADS * DH
    NEXP = expert_down.shape[0]
    KD = D // P
    NI = B * S // BLK
    CH = INNER // P
    KJ = PM + SEG
    NG = W * HEADS // 4
    HS = EH * 2
    NC = EH * TOP
    LO = NEXP // P
    assert D == 256 and DH == 64 and HEADS == 16 and KJ * 2 <= BANK and NC == 64 and LO == 32 and NK == 64
    assert DK == P and PM * 8 == P
    ROOT = float(DH) ** -0.5

    x_blk = x.rearrange("b s d -> (b s) d").rearrange("(n w p) d -> n p w d", w=W, p=P)
    out_blk = out.rearrange("b s d -> (b s) d").rearrange("(n w p) d -> n p w d", w=W, p=P)
    z_scratch = nc.dram_tensor("z_scratch", [NI, P, 2 * KD * BLK], F32, kind="Internal").ap()
    tab_scratch = nc.dram_tensor("tab_scratch", [W * (NI + 1), P, 3 * 64], F32, kind="Internal").ap()

    with ExitStack() as whole:
        def sem(name):
            return whole.enter_context(nc.semaphore(name))

        def shared(name, shape, dt):
            return whole.enter_context(nc.sbuf_tensor(name, shape, dt))

        ident = shared("ident", [P, P], F32)
        identb = shared("identb", [P, P], BF16)
        gam = shared("gam", [P, KD], F32)
        nrm = shared("nrm", [P, KD], F32)
        upw = shared("upw", [P, LO, D], F32)
        unscale = shared("unscale", [P, W * NI], F32)
        raw = upw[:].rearrange("p a b -> p (a b)")

        c_ident = sem("c_ident")
        c_mask = sem("c_mask")
        c_iota = sem("c_iota")
        d_small = sem("d_small")

        with ExitStack() as ctx:
            def sb(name, shape, dt):
                return ctx.enter_context(nc.sbuf_tensor(name, shape, dt))

            def ps(name, shape, dt=F32):
                return ctx.enter_context(nc.psum_tensor(name, shape, dt))

            maskneg = sb("maskneg", [P, KJ], BF16)
            iota8 = sb("iota8", [P, TOP], F32)
            minus_half = sb("minus_half", [P, W], F32)
            eps = sb("eps", [P, 2, W], F32)
            one = sb("one", [P, 1], F32)
            wqkv_h = sb("wqkv_h", [P, KD, 3 * INNER], F32R)
            wqkv_l = sb("wqkv_l", [P, KD, 3 * INNER], F32R)
            wsc_h = sb("wsc_h", [P, KD, HS * NK], F32R)
            wsc_l = sb("wsc_l", [P, KD, HS * NK], F32R)
            wout = sb("wout", [P, CH, D], F32)
            pmk2 = sb("pmk2", [P, 2, 2 * DH], F32)
            pmv_bd = sb("pmv_bd", [P, 2, 8 * DH], F32)
            xin = sb("xin", [P, W, D], F32)
            xres = sb("xres", [P, W, D], F32)
            stats = sb("stats", [P, W, 6], F32)
            mv = sb("mv", [P, W, 2], F32)
            rr = sb("rr", [P, 6, W], F32)
            z = sb("z", [P, W, D], F32)
            zhl = sb("zhl", [P, 2, KD, BLK], F32R)
            qT = sb("qT", [P, CH, BLK], F32)
            kT = sb("kT", [P, CH, W, KJ], F32)
            v = sb("v", [P, W, INNER], F32)
            sc = sb("sc", [P, W, HS * NK], F32)
            prob = [sb(f"prob{n}", [P, 8, KJ], F32) for n in range(2)]
            probT = [sb(f"probT{n}", [P, 4, P], F32) for n in range(2)]
            probpm = sb("probpm", [P, 2, 8, PM], F32)
            pmT = sb("pmT", [P, 2, P], F32)
            negmax = sb("negmax", [P, NG, 2, 2], F32)
            rowsum = sb("rowsum", [P, NG, 4], F32)
            recip = sb("recip", [P, 8], F32)
            o = sb("o", [P, INNER], F32)
            oT = sb("oT", [P, CH, P], F32)
            y = sb("y", [P, W, D], F32)
            top = sb("top", [P, HS, TOP], F32)
            topi = sb("topi", [P, HS, TOP], U32)
            topf = sb("topf", [P, HS, TOP], F32)
            cand = sb("cand", [P, EH, TOP, TOP], F32)
            best = sb("best", [P, NC], F32)
            besti = sb("besti", [P, NC], U32)
            rank = sb("rank", [P, 2, NC], U32)
            pick = sb("pick", [P, NC, TOP], F32)
            prod = sb("prod", [P, NC, TOP], F32)
            big = sb("big", [P, 5], F32)
            spare = sb("spare", [P, 1], F32)
            keyi = sb("keyi", [P, 2, NC], F32)
            high = sb("high", [P, NC], F32)
            tab = sb("tab", [P, W, 3, 2, NC], F32)
            tabT = sb("tabT", [P, W, 3, NC], F32)

            aux = [ps(f"aux{n}", [P, BANK]) for n in range(2)]
            sim = [ps(f"sim{n}", [P, 2, BANK]) for n in range(2)]
            ptb = ps("ptb", [P, 4, P])
            pvb = ps("pvb", [P, BANK])

            d_raw = sem("d_raw")
            d_wq = sem("d_wq")
            d_pmv = sem("d_pmv")
            d_wout = sem("d_wout")
            c_pmv0 = sem("c_pmv0")
            c_roots = sem("c_roots")
            set_ps = sem("set_ps")
            set_ev = sem("set_ev")
            w_hi = sem("w_hi")
            w_split = sem("w_split")
            d_xin = sem("d_xin")
            d_xres = sem("d_xres")
            st_z = sem("st_z")
            st_tab = [sem(f"st_tab{w}") for w in range(W)]
            st_y = [sem(f"st_y{w}") for w in range(W)]
            ln_bn = sem("ln_bn")
            ln_mv = sem("ln_mv")
            ln_step = sem("ln_step")
            ln_r = sem("ln_r")
            z_ready = sem("z_ready")
            z_hi = sem("z_hi")
            aux_full = sem("aux_full")
            aux_act = sem("aux_act")
            aux_dve = sem("aux_dve")
            qk_done = sem("qk_done")
            max_done = sem("max_done")
            exp_done = sem("exp_done")
            pm_packed = sem("pm_packed")
            pt_done = sem("pt_done")
            pt_ev = sem("pt_ev")
            pv_done = sem("pv_done")
            rcp = sem("rcp")
            norm_done = sem("norm_done")
            t_top = sem("t_top")
            t_topi = sem("t_topi")
            t_topf = sem("t_topf")
            t_cand = sem("t_cand")
            t_best = sem("t_best")
            t_scale = sem("t_scale")
            t_inv = sem("t_inv")
            t_besti = sem("t_besti")
            t_rank = sem("t_rank")
            t_pick = sem("t_pick")
            t_prod = sem("t_prod")
            t_key = sem("t_key")
            t_high = sem("t_high")
            tab_ready = sem("tab_ready")

            USES = ([(f"qk{m}", "A") for m in range(8)] + [(f"v{m}", "A") for m in range(4)]
                    + [("tab0", "D"), ("pm0", "D"), ("sc0", "A"), ("sc1", "A"), ("pm1", "D"), ("sc2", "A"),
                       ("sc3", "A"), ("pm2", "D"), ("oT0", "A"), ("oT1", "A"), ("zT0", "D"), ("zT1", "D"),
                       ("wo0", "D"), ("pm3", "D"), ("tab1", "D"), ("oT2", "A"), ("oT3", "A"), ("wo1", "D")])
            NU = len(USES)
            UI = {name: n for n, (name, _) in enumerate(USES)}
            NA = sum(e == "A" for _, e in USES)
            ND = NU - NA
            assert NU % 2 == 0

            def emptied(name):
                u = UI[name]
                who = USES[u][1]
                return who, sum(e == who for _, e in USES[:u + 1])

            def wait_emptied(eng, i, name):
                who, n = emptied(name)
                eng.wait_ge(aux_act if who == "A" else aux_dve, i * (NA if who == "A" else ND) + n)

            def bank(name):
                return aux[UI[name] % 2]

            def split3(pe, outp, wh, wl, xh, xl, first, last):
                pe.matmul(outp, wl, xh, start=first, stop=False)
                pe.matmul(outp, wh, xl, start=False, stop=False)
                return pe.matmul(outp, wh, xh, start=False, stop=last)

            block = ctx.enter_context(nc.Block())

            @block.sync
            def _(sp):
                sp.dma_start(xin[:], x_blk[0]).then_inc(d_xin, 16)
                sp.dma_start(gam[:], gamma.rearrange("(k p) -> p k", p=P), allow_slow_non_contiguous=True).then_inc(d_small, 16)
                sp.dma_start(nrm[:], norm_w.rearrange("(k p) -> p k", p=P), allow_slow_non_contiguous=True).then_inc(d_small, 16)
                pmk_rows = pm_k.rearrange("(a h) p d -> (h p) a d", a=2)
                for copy in range(2):
                    sp.dma_start(pmk2[:, :, copy * DH:(copy + 1) * DH], pmk_rows).then_inc(d_small, 16)
                sp.dma_start(raw[:, 0:KD * 3 * INNER].rearrange("p (k n) -> p k n", k=KD),
                             w_qkv.rearrange("(k p) n -> p k n", p=P)).then_inc(d_raw, 16)
                sp.dma_start(raw[0:NK, KD * 3 * INNER:].rearrange("p (h n) -> p h n", h=EH),
                             keys.rearrange("h k s d -> k h (s d)")).then_inc(d_wq, 16)
                wq_rows = w_q.rearrange("(m p) d -> p m d", p=P)
                sp.dma_start(v[:].rearrange("p w (m d) -> p (w m) d", d=D), wq_rows[:, 0:8]).then_inc(d_wq, 16)
                sp.dma_start(sc[:].rearrange("p w (m d) -> p (w m) d", d=D), wq_rows[:, 8:16]).then_inc(d_wq, 16)
                sp.dma_start(wout[:], w_out.rearrange("(c p) n -> p c n", p=P)).then_inc(d_wout, 16)
                sp.wait_ge(c_pmv0, 1)
                for hh in range(8):
                    sp.dma_start(pmv_bd[hh * PM:(hh + 1) * PM, :, hh * DH:(hh + 1) * DH],
                                 pm_v.rearrange("(a h) p d -> h p a d", a=2)[hh]).then_inc(d_pmv, 16)

                def store_z(i):
                    sp.dma_start(z_scratch[i], zhl[:].rearrange("p a k t -> p (a k t)").bitcast(F32)).then_inc(st_z, 16)

                def body(i, first, last):
                    sp.wait_ge(z_ready, W * i + W)
                    sp.dma_start(xin[:], x_blk[NI - 1 if last else i + 1]).then_inc(d_xin, 16)
                    if not first:
                        wait_emptied(sp, i - 1, "wo1")
                    sp.dma_start(xres[:], x_blk[i]).then_inc(d_xres, 16)
                    wait_emptied(sp, i, "tab0")
                    sp.dma_start(tab_scratch[W * i], tabT[:, 0].rearrange("p a q -> p (a q)")).then_inc(st_tab[0], 16)
                    if not last:
                        wait_emptied(sp, i, "zT1")
                        store_z(i + 1)
                    wait_emptied(sp, i, "wo0")
                    sp.dma_start(out_blk[i, :, 0], y[:, 0]).then_inc(st_y[0], 16)
                    wait_emptied(sp, i, "tab1")
                    sp.dma_start(tab_scratch[W * i + 1], tabT[:, 1].rearrange("p a q -> p (a q)")).then_inc(st_tab[1], 16)
                    wait_emptied(sp, i, "wo1")
                    sp.dma_start(out_blk[i, :, 1], y[:, 1]).then_inc(st_y[1], 16)

                sp.wait_ge(set_ev, 9)
                store_z(0)
                body(0, True, False)
                sp.wait_ge(w_split, KD)
                sp.dma_start(upw[:], expert_up.rearrange("(p c) d -> p c d", c=LO)).then_inc(d_small, 16)
                with sp.Fori(1, NI - 1) as i:
                    body(i, False, False)
                body(NI - 1, False, True)
                for w in range(W):
                    sp.wait_ge(aux_dve, NI * ND + w + 1)
                    sp.dma_start(tab_scratch[W * NI + w], tabT[:, w].rearrange("p a q -> p (a q)")).then_inc(st_tab[w], 16)
                sp.wait_ge(st_z, 16 * NI)
                for w in range(W):
                    sp.wait_ge(st_tab[w], 16 * (NI + 1))
                    sp.wait_ge(st_y[w], 16 * NI)
                sp.wait_ge(d_small, 16 * 5)

            @block.gpsimd
            def _(pool):
                pool.memset(ident[:], 0.0).then_inc(c_ident, 1)
                pool.wait_ge(c_ident, 1)
                pool.affine_select(out=ident[:], in_=ident[:], compare_op=ALU.not_equal, fill=1.0, base=0,
                                   pattern=[[-1, P]], channel_multiplier=1).then_inc(c_ident, 1)
                pool.memset(minus_half[:], -0.5).then_inc(c_roots, 1)
                pool.memset(eps[:, 0], 1e-5).then_inc(c_roots, 1)
                pool.memset(eps[:, 1], 1e-6).then_inc(c_roots, 1)
                pool.memset(one[:], 1.0).then_inc(c_roots, 1)
                pool.memset(pmv_bd[:], 0.0).then_inc(c_pmv0, 1)
                for w in range(W):
                    pool.memset(tab[:, w], 0.0).then_inc(tab_ready, 1)
                pool.memset(identb[:], 0.0).then_inc(c_mask, 1)
                pool.memset(maskneg[:], 0.0).then_inc(c_mask, 1)
                pool.wait_ge(c_mask, 2)
                pool.affine_select(out=identb[:], in_=identb[:], compare_op=ALU.not_equal, fill=1.0, base=0,
                                   pattern=[[-1, P]], channel_multiplier=1).then_inc(c_mask, 1)
                pool.affine_select(out=maskneg[:, PM:KJ], in_=maskneg[:, PM:KJ], compare_op=ALU.is_ge, fill=-1e37,
                                   base=0, pattern=[[-1, SEG]], channel_multiplier=1).then_inc(c_mask, 1)
                pool.iota(iota8[:], pattern=[[1, TOP]], base=0, channel_multiplier=0,
                          allow_small_or_imprecise_dtypes=True).then_inc(c_iota, 1)

                def roots(i):
                    b = 6 * i
                    pool.wait_ge(ln_mv, W * i + W)
                    pool.tensor_tensor(out=rr[:, 0], in0=mv[:, :, 1], in1=eps[:, 0], op=ALU.add).then_inc(ln_step, 1)
                    pool.wait_ge(ln_step, b + 1)
                    pool.tensor_tensor(out=rr[:, 1], in0=rr[:, 0], in1=minus_half[:], op=ALU.pow).then_inc(ln_step, 1)
                    pool.wait_ge(ln_step, b + 2)
                    pool.tensor_tensor(out=rr[:, 2], in0=rr[:, 1], in1=rr[:, 1], op=ALU.mult).then_inc(ln_step, 1)
                    pool.wait_ge(ln_step, b + 3)
                    pool.tensor_tensor(out=rr[:, 3], in0=rr[:, 2], in1=mv[:, :, 1], op=ALU.mult).then_inc(ln_step, 1)
                    pool.wait_ge(ln_step, b + 4)
                    pool.tensor_tensor(out=rr[:, 2], in0=rr[:, 3], in1=eps[:, 1], op=ALU.add).then_inc(ln_step, 1)
                    pool.wait_ge(ln_step, b + 5)
                    pool.tensor_tensor(out=rr[:, 4], in0=rr[:, 2], in1=minus_half[:], op=ALU.pow).then_inc(ln_step, 1)
                    pool.wait_ge(ln_step, b + 6)
                    pool.tensor_tensor(out=rr[:, 5], in0=rr[:, 4], in1=rr[:, 1], op=ALU.mult).then_inc(ln_r, 1)

                def body(i):
                    for half in range(4):
                        if half == 2:
                            roots(i + 1)
                        pool.wait_ge(exp_done, NG * i + 2 * half + 2)
                        if half >= 2:
                            pool.wait_ge(aux_full, NU * i + UI[f"pm{half - 2}"] + 1)
                        pool.tensor_tensor(out=probpm[:, half % 2], in0=prob[half % 2][:, :, 0:PM],
                                           in1=one[:].unsqueeze(2).broadcast_to([P, 8, PM]),
                                           op=ALU.mult).then_inc(pm_packed, 1)

                pool.wait_ge(c_roots, 4)
                roots(0)
                body(0)
                with pool.Fori(1, NI) as i:
                    body(i)

            @block.scalar
            def _(act):
                act.preload_act_table(ACT.Exp)

                def empty(i, name, outp, inp, scale=1.0):
                    act.wait_ge(aux_full, NU * i + UI[name] + 1)
                    act.activation(outp, inp, ACT.Copy, scale=scale).then_inc(aux_act, 1)

                def body(i, first):
                    for m in range(4):
                        empty(i, f"qk{m}", qT[:, 2 * m:2 * m + 2, :],
                              bank(f"qk{m}")[:].rearrange("p (c t) -> p c t", c=2), scale=ROOT)
                    for m in range(4):
                        empty(i, f"qk{4 + m}", kT[:, 2 * m:2 * m + 2, :, PM:KJ],
                              bank(f"qk{4 + m}")[:].rearrange("p (c w t) -> p c w t", c=2, w=W))

                    def empty_v(m):
                        empty(i, f"v{m}", v[:, m // 2, (m % 2) * BANK:(m % 2 + 1) * BANK], bank(f"v{m}")[:])

                    empty_v(0)
                    empty_v(1)

                    def empty_sc(m):
                        if m % 2 == 0 and not first:
                            act.wait_ge(t_topi, W * i + m // 2 - 1)
                        empty(i, f"sc{m}", sc[:, m // 2, (m % 2) * BANK:(m % 2 + 1) * BANK], bank(f"sc{m}")[:])

                    def empty_oT(m):
                        empty(i, f"oT{m}", oT[:, 4 * (m % 2):4 * (m % 2) + 4, :],
                              bank(f"oT{m}")[:].rearrange("p (c t) -> p c t", c=4))

                    for n in range(NG):
                        act.wait_ge(max_done, NG * i + n + 1)
                        if n % 2 == 0 and (n >= 4 or not first):
                            act.wait_ge(pm_packed, 4 * i + n // 2 - 1)
                        for j in range(2):
                            for par in range(2):
                                slot = 4 * (n % 2) + 2 * j + par
                                last = act.activation(
                                    prob[n // 2 % 2][:, slot, :], sim[n % 2][:, par, j * KJ:(j + 1) * KJ], ACT.Exp,
                                    bias=negmax[:, n, par, j:j + 1], scale=1.0,
                                    accum_out=rowsum[:, n, 2 * j + par:2 * j + par + 1])
                        last.then_inc(exp_done, 1)
                        if n < 2:
                            empty_v(2 + n)
                        elif n < 6:
                            empty_sc(n - 2)
                        elif n == 6:
                            empty_oT(0)
                            empty_oT(1)
                        act.wait_ge(pt_done, NG * i + n + 1)
                        act.activation(probT[n % 2][:], ptb[:], ACT.Copy).then_inc(pt_ev, 1)
                    empty_oT(2)
                    empty_oT(3)

                body(0, True)
                with act.Fori(1, NI) as i:
                    body(i, False)

            @block.vector
            def _(dve):
                dve.wait_ge(d_small, 16 * 4)
                dve.wait_ge(d_raw, 16)
                for k in range(KD):
                    rw = raw[:, k * 3 * INNER:(k + 1) * 3 * INNER]
                    dve.tensor_scalar(out=wqkv_h[:, k], in0=rw, scalar1=gam[:, k:k + 1], scalar2=None,
                                      op0=ALU.mult).then_inc(w_hi, 1)
                    dve.wait_ge(w_hi, k + 1)
                    dve.scalar_tensor_tensor(out=wqkv_l[:, k], in0=rw, scalar=gam[:, k:k + 1],
                                             in1=wqkv_h[:, k].bitcast(F32), op0=ALU.mult,
                                             op1=ALU.subtract).then_inc(w_split, 1)
                dve.wait_ge(set_ps, 1)
                for half in range(2):
                    rows = aux[0][:, half * P:(half + 1) * P].rearrange("p (c e s) -> p c e s", e=2, s=PM)
                    for par in range(2):
                        for w in range(W):
                            last = dve.tensor_copy(kT[par * DH:(par + 1) * DH, 4 * half:4 * half + 4, w, 0:PM],
                                                   rows[par * DH:(par + 1) * DH, :, par, :])
                last.then_inc(set_ev, 1)
                for n in range(2):
                    dve.wait_ge(set_ps, 2 + n)
                    dve.tensor_copy(o[:, n * BANK:(n + 1) * BANK], aux[(1 + n) % 2][:]).then_inc(set_ev, 1)
                for k in range(KD):
                    for n in range(2):
                        u = 3 + 2 * k + n
                        dve.wait_ge(set_ps, u + 1)
                        hi = wsc_h[:, k, n * BANK:(n + 1) * BANK]
                        dve.tensor_scalar(out=hi, in0=aux[u % 2][:], scalar1=nrm[:, k:k + 1], scalar2=None,
                                          op0=ALU.mult).then_inc(w_hi, 1)
                        dve.wait_ge(w_hi, KD + 2 * k + n + 1)
                        dve.scalar_tensor_tensor(out=wsc_l[:, k, n * BANK:(n + 1) * BANK], in0=aux[u % 2][:],
                                                 scalar=nrm[:, k:k + 1], in1=hi.bitcast(F32), op0=ALU.mult,
                                                 op1=ALU.subtract).then_inc(set_ev, 1)

                def moments(i):
                    dve.wait_ge(d_xin, 16 * i + 16)
                    for w in range(W):
                        dve.bn_stats(stats[:, w], xin[:, w]).then_inc(ln_bn, 1)

                def aggregate():
                    for w in range(W):
                        dve.bn_aggr(mv[:, w], stats[:, w]).then_inc(ln_mv, 1)

                def normed(i, first=False):
                    dve.wait_ge(ln_r, i + 1)
                    dve.wait_ge(ln_mv, W * i + W)
                    for w in range(W):
                        dve.tensor_scalar(out=z[:, w], in0=xin[:, w], scalar1=mv[:, w, 0:1],
                                          scalar2=rr[:, 5, w:w + 1], op0=ALU.subtract,
                                          op1=ALU.mult).then_inc(z_ready, 1)

                def split_z(w, b, count, done):
                    src = b[:, 0:KD * P].rearrange("p (k t) -> p k t", k=KD)
                    hi = zhl[:, 0, :, w * P:(w + 1) * P]
                    dve.tensor_copy(hi, src).then_inc(z_hi, 1)
                    dve.wait_ge(z_hi, count)
                    dve.tensor_tensor(out=zhl[:, 1, :, w * P:(w + 1) * P], in0=src, in1=hi.bitcast(F32),
                                      op=ALU.subtract).then_inc(done, 1)

                def choose(t, w):
                    s3 = sc[:, w].rearrange("p (m k) -> p m k", k=NK)

                    def tops(m0):
                        for m in range(m0, m0 + 8):
                            last = dve.max(top[:, m], s3[:, m])
                        if m0 == 8:
                            last.then_inc(t_top, 1)

                    def pairs():
                        dve.wait_ge(t_top, t + 1)
                        a = top[:].rearrange("p (h s) k -> p h s k", s=2)
                        dve.tensor_tensor(
                            out=cand[:], in0=a[:, :, 0, :].unsqueeze(3).broadcast_to([P, EH, TOP, TOP]),
                            in1=a[:, :, 1, :].unsqueeze(2).broadcast_to([P, EH, TOP, TOP]),
                            op=ALU.add).then_inc(t_cand, 1)

                    def topis(m0):
                        for m in range(m0, m0 + 8):
                            last = dve.max_index(topi[:, m], top[:, m], s3[:, m])
                        if m0 == 8:
                            last.then_inc(t_topi, 1)

                    def bests():
                        dve.wait_ge(t_topi, t + 1)
                        dve.wait_ge(t_cand, t + 1)
                        dve.tensor_copy(topf[:], topi[:]).then_inc(t_topf, 1)
                        for h in range(EH):
                            last = dve.max(best[:, h * TOP:(h + 1) * TOP], cand[:, h].rearrange("p a b -> p (a b)"))
                        last.then_inc(t_best, 1)

                    def scale():
                        dve.wait_ge(t_best, t + 1)
                        dve.tensor_reduce(out=big[:, 0:1], in_=best[:], axis=AX.X, op=ALU.max).then_inc(t_scale, 1)
                        dve.wait_ge(t_scale, 4 * t + 1)
                        dve.tensor_scalar(out=big[:, 1:2], in0=big[:, 0:1], scalar1=2.0 ** -100, scalar2=None,
                                          op0=ALU.max).then_inc(t_scale, 1)
                        dve.wait_ge(t_scale, 4 * t + 2)
                        dve.tensor_scalar(out=big[:, 2:3].bitcast(U32), in0=big[:, 1:2].bitcast(U32),
                                          scalar1=0x7F800000, scalar2=None, op0=ALU.bitwise_and).then_inc(t_scale, 1)
                        dve.wait_ge(t_scale, 4 * t + 3)
                        dve.tensor_scalar(out=big[:, 3:4], in0=big[:, 2:3], scalar1=2.0 ** -14, scalar2=None,
                                          op0=ALU.mult).then_inc(t_scale, 1)
                        dve.wait_ge(t_scale, 4 * t + 4)
                        dve.tensor_copy(unscale[:, bass.ds(t, 1)], big[:, 3:4])
                        dve.reciprocal(big[:, 4:5], big[:, 3:4]).then_inc(t_inv, 1)

                    def twice(a):
                        return a.unsqueeze(1).broadcast_to([P, 2, NC])

                    def bestis():
                        dve.wait_ge(t_inv, t + 1)
                        dve.tensor_scalar(out=tab[:, w, 2], in0=twice(best[:]), scalar1=0.0, scalar2=big[:, 4:5],
                                          op0=ALU.max, op1=ALU.mult)
                        for h in range(EH):
                            last = dve.max_index(besti[:, h * TOP:(h + 1) * TOP], best[:, h * TOP:(h + 1) * TOP],
                                                 cand[:, h].rearrange("p a b -> p (a b)"))
                        last.then_inc(t_besti, 1)

                    def ranks():
                        dve.wait_ge(t_besti, t + 1)
                        dve.tensor_scalar(out=rank[:, 0], in0=besti[:], scalar1=3, scalar2=None,
                                          op0=ALU.logical_shift_right)
                        dve.tensor_scalar(out=rank[:, 1], in0=besti[:], scalar1=7, scalar2=None,
                                          op0=ALU.bitwise_and).then_inc(t_rank, 1)

                    def lookup(s):
                        if s == 1:
                            dve.wait_ge(t_key, 2 * t + 1)
                        if s == 0:
                            dve.wait_ge(t_rank, t + 1)
                            dve.wait_ge(t_topf, t + 1)
                        dve.tensor_tensor(out=pick[:], in0=rank[:, s].unsqueeze(2).broadcast_to([P, NC, TOP]),
                                          in1=iota8[:].unsqueeze(1).broadcast_to([P, NC, TOP]),
                                          op=ALU.is_equal).then_inc(t_pick, 1)
                        dve.wait_ge(t_pick, 2 * t + s + 1)
                        f = topf[:].rearrange("p (h s) k -> p h s k", s=2)[:, :, s, :]
                        dve.tensor_tensor(
                            out=prod[:].rearrange("p (h c) a -> p h c a", c=TOP),
                            in0=pick[:].rearrange("p (h c) a -> p h c a", c=TOP),
                            in1=f.unsqueeze(2).broadcast_to([P, EH, TOP, TOP]), op=ALU.mult).then_inc(t_prod, 1)
                        dve.wait_ge(t_prod, 2 * t + s + 1)
                        dve.tensor_reduce(out=keyi[:, s], in_=prod[:], axis=AX.X, op=ALU.add).then_inc(t_key, 1)

                    def table():
                        dve.wait_ge(t_key, 2 * t + 2)
                        dve.tensor_scalar(out=high[:], in0=keyi[:, 1], scalar1=float(LO), scalar2=None,
                                          op0=ALU.is_ge).then_inc(t_high, 1)
                        dve.wait_ge(t_high, t + 1)
                        dve.scalar_tensor_tensor(out=tab[:, w, 0], in0=twice(keyi[:, 0]), scalar=float(NK // LO),
                                                 in1=twice(high[:]), op0=ALU.mult, op1=ALU.add)
                        dve.scalar_tensor_tensor(out=tab[:, w, 1], in0=twice(high[:]), scalar=-float(LO),
                                                 in1=twice(keyi[:, 1]), op0=ALU.mult,
                                                 op1=ALU.add).then_inc(tab_ready, 1)

                    return [lambda: tops(0), lambda: tops(8), pairs, lambda: topis(0), lambda: topis(8), bests,
                            scale, bestis, ranks, lambda: lookup(0), lambda: lookup(1), table]

                def empty_tab(i, w, first):
                    if not first:
                        dve.wait_ge(st_tab[w], 16 * i)
                    dve.wait_ge(aux_full, NU * i + UI[f"tab{w}"] + 1)
                    src = bank(f"tab{w}")[:, 0:3 * P].rearrange("p (a t) -> p a t", a=3)
                    dve.tensor_copy(tabT[0:64, w], src[0:64, :, 0:64])
                    dve.tensor_copy(tabT[64:128, w], src[64:128, :, 64:128]).then_inc(aux_dve, 1)

                def body(i, first):
                    later = []
                    if not first:
                        wait_emptied(dve, i - 1, "sc3")
                        dve.wait_ge(tab_ready, W * i)
                        dve.memset(spare[:], 0.0)
                        for piece in choose(W * i - W, 0):
                            piece()
                        later = choose(W * i - W + 1, 1)

                    def maxima(n):
                        dve.wait_ge(qk_done, NG * i + n + 1)
                        dve.tensor_reduce(out=negmax[:, n], in_=sim[n % 2][:, :, 0:2 * KJ].rearrange(
                            "p e (j k) -> p e j k", k=KJ), axis=AX.X, op=ALU.max, negate=True).then_inc(max_done, 1)

                    def empty_pm(half):
                        dve.wait_ge(aux_full, NU * i + UI[f"pm{half}"] + 1)
                        dve.tensor_copy(pmT[:, half % 2], bank(f"pm{half}")[:, 0:P]).then_inc(aux_dve, 1)

                    def normalise(half):
                        dve.wait_ge(exp_done, NG * i + 2 * half + 2)
                        if half > 0 or not first:
                            dve.wait_ge(norm_done, 4 * i + half)
                        dve.reciprocal(recip[:], rowsum[:, 2 * half:2 * half + 2].rearrange("p a b -> p (a b)")
                                       ).then_inc(rcp, 1)
                        dve.wait_ge(rcp, 4 * i + half + 1)
                        dve.wait_ge(pv_done, 4 * i + half + 1)
                        dve.tensor_tensor(
                            out=o[:, (half % 2) * BANK:(half % 2 + 1) * BANK].rearrange("p (h d) -> p h d", d=DH),
                            in0=pvb[:].rearrange("p (h d) -> p h d", d=DH),
                            in1=recip[:].unsqueeze(2).broadcast_to([P, 8, DH]), op=ALU.mult).then_inc(norm_done, 1)

                    def add_x(w):
                        if w == 0:
                            dve.wait_ge(d_xres, 16 * i + 16)
                        if not first:
                            dve.wait_ge(st_y[w], 16 * i)
                        dve.wait_ge(aux_full, NU * i + UI[f"wo{w}"] + 1)
                        dve.tensor_tensor(out=y[:, w], in0=bank(f"wo{w}")[:, 0:D], in1=xres[:, w],
                                          op=ALU.add).then_inc(aux_dve, 1)

                    maxima(0)
                    for n in range(NG):
                        if n == 3:
                            dve.wait_ge(ln_bn, W * i + 2 * W)
                        if n == 0 and later:
                            dve.wait_ge(tab_ready, W * i + 1)
                        if n + 1 < NG:
                            maxima(n + 1)
                        if n == 3:
                            aggregate()
                        if n == 1:
                            empty_tab(i, 0, first)
                        if n == 7:
                            dve.wait_ge(st_z, 16 * i + 16)
                            for w in range(W):
                                dve.wait_ge(aux_full, NU * i + UI[f"zT{w}"] + 1)
                                split_z(w, bank(f"zT{w}"), W * i + W + w + 1, aux_dve)
                            add_x(0)
                        if n % 2 == 1:
                            empty_pm(n // 2)
                        if n >= 2 and n % 2 == 0:
                            normalise(n // 2 - 1)
                        if n == 2:
                            moments(i + 1)
                        if n == 5:
                            normed(i + 1)
                        for piece in later[2 * n:2 * n + 2]:
                            piece()
                    empty_tab(i, 1, first)
                    normalise(3)
                    add_x(1)

                moments(0)
                dve.wait_ge(ln_bn, W)
                aggregate()
                normed(0)
                for w in range(W):
                    dve.wait_ge(set_ps, 8 + w)
                    split_z(w, aux[(7 + w) % 2], w + 1, set_ev)
                dve.wait_ge(c_iota, 1)
                body(0, True)
                with dve.Fori(1, NI) as i:
                    body(i, False)
                for w in range(W):
                    wait_emptied(dve, NI - 1, f"sc{2 * w + 1}")
                    dve.wait_ge(tab_ready, W * NI + w)
                    for piece in choose(W * (NI - 1) + w, w):
                        piece()
                for w in range(W):
                    dve.wait_ge(st_tab[w], 16 * NI)
                    dve.wait_ge(aux_full, NU * NI + w + 1)
                    src = aux[w][:, 0:3 * P].rearrange("p (a t) -> p a t", a=3)
                    dve.tensor_copy(tabT[0:64, w], src[0:64, :, 0:64])
                    dve.tensor_copy(tabT[64:128, w], src[64:128, :, 64:128]).then_inc(aux_dve, 1)

            @block.tensor
            def _(pe):
                pe.wait_ge(c_ident, 2)
                pe.wait_ge(d_small, 16 * 4)
                for half in range(2):
                    last = pe.transpose(aux[0][:, half * P:(half + 1) * P], pmk2[:, half], ident[:])
                last.then_inc(set_ps, 1)
                pe.wait_ge(d_wq, 16 * 3)
                keyrows = raw[0:NK, KD * 3 * INNER:].rearrange("p (m d) -> p m d", d=DK)
                for n in range(2):
                    if n == 1:
                        pe.wait_ge(set_ev, 1)
                    for m in range(8):
                        last = pe.transpose(aux[(1 + n) % 2][:, m * NK:(m + 1) * NK], keyrows[:, 8 * n + m],
                                            ident[0:NK, 0:NK])
                    last.then_inc(set_ps, 1)
                for k in range(KD):
                    for n in range(2):
                        u = 3 + 2 * k + n
                        pe.wait_ge(set_ev, 3 if u == 3 else u - 1)
                        rows = (v if n == 0 else sc)[:].rearrange("p w (m d) -> p (w m) d", d=D)
                        for m in range(8):
                            last = pe.matmul(aux[u % 2][:, m * NK:(m + 1) * NK], rows[:, m, k * P:(k + 1) * P],
                                             o[:, (8 * n + m) * NK:(8 * n + m + 1) * NK], start=True, stop=True)
                        last.then_inc(set_ps, 1)
                pe.wait_ge(z_ready, W)
                for w in range(W):
                    pe.wait_ge(set_ev, 6 + w)
                    for k in range(KD):
                        last = pe.transpose(aux[(7 + w) % 2][:, k * P:(k + 1) * P], z[:, w, k * P:(k + 1) * P], ident[:])
                    last.then_inc(set_ps, 1)
                pe.wait_ge(set_ev, 9)
                pe.wait_ge(w_split, KD)
                pe.wait_ge(c_mask, 4)

                def use(i, name, first):
                    u = UI[name]
                    if u >= 2:
                        wait_emptied(pe, i, USES[u - 2][0])
                    elif not first:
                        wait_emptied(pe, i - 1, USES[u - 2][0])
                    return bank(name)

                def body(i, first):
                    if not first:
                        wait_emptied(pe, i - 1, "zT1")

                    def transpose_z():
                        pe.wait_ge(z_ready, W * i + 2 * W)
                        for w in range(W):
                            b = use(i, f"zT{w}", first)
                            for k in range(KD):
                                last = pe.transpose(b[:, k * P:(k + 1) * P], z[:, w, k * P:(k + 1) * P], ident[:])
                            last.then_inc(aux_full, 1)

                    for m in range(8):
                        b = use(i, f"qk{m}", first)
                        for c in range(2):
                            cols = slice((2 * m + c) * P, (2 * m + c + 1) * P)
                            for k in range(KD):
                                last = split3(pe, b[:, c * BLK:(c + 1) * BLK], wqkv_h[:, k, cols], wqkv_l[:, k, cols],
                                              zhl[:, 0, k], zhl[:, 1, k], k == 0, k == KD - 1)
                        last.then_inc(aux_full, 1)

                    def rows_times(name, wh, wl, w, n0):
                        b = use(i, name, first)
                        tok = slice(w * P, (w + 1) * P)
                        for k in range(KD):
                            last = split3(pe, b[:], zhl[:, 0, k, tok], zhl[:, 1, k, tok], wh[:, k, n0:n0 + BANK],
                                          wl[:, k, n0:n0 + BANK], k == 0, k == KD - 1)
                        last.then_inc(aux_full, 1)

                    def values(m):
                        rows_times(f"v{m}", wqkv_h, wqkv_l, m // 2, 2 * INNER + (m % 2) * BANK)

                    values(0)
                    values(1)

                    def scores(m):
                        rows_times(f"sc{m}", wsc_h, wsc_l, m // 2, (m % 2) * BANK)

                    def qk(n):
                        w = n // 4
                        if n >= 2:
                            pe.wait_ge(exp_done, NG * i + n - 1)
                        elif not first:
                            pe.wait_ge(exp_done, NG * i + n - 1)
                        if n == 0:
                            wait_emptied(pe, i, "qk7")
                        for par in range(2):
                            pe.matmul(sim[n % 2][:, par, 0:2 * KJ].rearrange("p (j k) -> p j k", k=KJ), identb[:],
                                      maskneg[:].unsqueeze(1).broadcast_to([P, 2, KJ]), start=True, stop=False)
                        for j in range(2):
                            for par in range(2):
                                c = 2 * (n % 4) + j
                                rows = slice(par * DH, (par + 1) * DH)
                                last = pe.matmul(sim[n % 2][:, par, j * KJ:(j + 1) * KJ],
                                                 qT[rows, c, w * P:(w + 1) * P], kT[rows, c, w, :],
                                                 start=False, stop=(j == 1))
                        last.then_inc(qk_done, 1)

                    def transpose_probs(n):
                        pe.wait_ge(exp_done, NG * i + n + 1)
                        if n >= 1 or not first:
                            pe.wait_ge(pt_ev, NG * i + n)
                        for hh in range(4):
                            last = pe.transpose(ptb[:, hh], prob[n // 2 % 2][:, 4 * (n % 2) + hh, PM:KJ], ident[:])
                        last.then_inc(pt_done, 1)

                    def transpose_pm(half):
                        b = use(i, f"pm{half}", first)
                        pe.wait_ge(pm_packed, 4 * i + half + 1)
                        pe.transpose(b[:, 0:P], probpm[:, half % 2].rearrange("p h s -> p (h s)"),
                                     ident[:]).then_inc(aux_full, 1)

                    def pv(n):
                        half = n // 2
                        if n % 4 == 0:
                            wait_emptied(pe, i, f"v{n // 4 * 2 + 1}")
                        if n % 2 == 0 and (half > 0 or not first):
                            pe.wait_ge(norm_done, 4 * i + half)
                        pe.wait_ge(pt_ev, NG * i + n + 1)
                        for hh in range(4):
                            head = 4 * (n % 4) + hh
                            slot = 4 * (n % 2) + hh
                            pe.matmul(pvb[:, slot * DH:(slot + 1) * DH], probT[n % 2][:, hh],
                                      v[:, n // 4, head * DH:(head + 1) * DH], start=(slot == 0), stop=False)
                        if n % 2 == 1:
                            wait_emptied(pe, i, f"pm{half}")
                            pe.matmul(pvb[:], pmT[:, half % 2], pmv_bd[:, half % 2], start=False,
                                      stop=True).then_inc(pv_done, 1)

                    def transpose_o(m):
                        b = use(i, f"oT{m}", first)
                        pe.wait_ge(norm_done, 4 * i + m + 1)
                        for c in range(4):
                            cc = 4 * (m % 2) + c
                            last = pe.transpose(b[:, c * P:(c + 1) * P], o[:, cc * P:(cc + 1) * P], ident[:])
                        last.then_inc(aux_full, 1)

                    def project(w):
                        b = use(i, f"wo{w}", first)
                        wait_emptied(pe, i, f"oT{2 * w + 1}")
                        for c in range(CH):
                            last = pe.matmul(b[:, 0:D], oT[:, c], wout[:, c], start=(c == 0), stop=(c == CH - 1))
                        last.then_inc(aux_full, 1)

                    def transpose_tab(w):
                        b = use(i, f"tab{w}", first)
                        pe.wait_ge(tab_ready, W * i + w + 1)
                        for a in range(3):
                            last = pe.transpose(b[:, a * P:(a + 1) * P], tab[:, w, a].rearrange("p e c -> p (e c)"),
                                                ident[:])
                        last.then_inc(aux_full, 1)

                    qk(0)
                    for n in range(NG):
                        if n + 1 < NG:
                            qk(n + 1)
                        if n < 2:
                            values(2 + n)
                        if n == 1:
                            transpose_tab(0)
                        if 2 <= n < 6:
                            scores(n - 2)
                        if n == 6:
                            transpose_o(0)
                            transpose_o(1)
                        if n == 7:
                            transpose_z()
                            project(0)
                        transpose_probs(n)
                        if n % 2 == 1:
                            transpose_pm(n // 2)
                        if n >= 1:
                            pv(n - 1)
                    transpose_tab(1)
                    pv(7)
                    transpose_o(2)
                    transpose_o(3)
                    project(1)

                pe.wait_ge(d_wout, 16)
                pe.wait_ge(d_pmv, 16 * 8)
                body(0, True)
                with pe.Fori(1, NI) as i:
                    body(i, False)
                for w in range(W):
                    wait_emptied(pe, NI - 1, USES[NU - 2 + w][0])
                    pe.wait_ge(tab_ready, W * NI + w + 1)
                    for a in range(3):
                        last = pe.transpose(aux[w][:, a * P:(a + 1) * P], tab[:, w, a].rearrange("p e c -> p (e c)"),
                                            ident[:])
                    last.then_inc(aux_full, 1)

        with ExitStack() as ctx:
            def sb(name, shape, dt):
                return ctx.enter_context(nc.sbuf_tensor(name, shape, dt))

            def ps(name, shape, dt=F32):
                return ctx.enter_context(nc.psum_tensor(name, shape, dt))

            UQ = 32
            NUN = BLK // 2 // UQ
            PC = 8
            NP = BLK // 2 // PC
            ND2 = LO // 2

            wd_h = sb("wd_h", [P, LO, KD, P], F32R)
            wd_l = sb("wd_l", [P, LO, KD, P], F32R)
            g = sb("g", [P, W + 1, LO, P], F32)
            down_raw = g[:].rearrange("p s c t -> p (s c t)")[:, 0:LO * D].rearrange("p (c d) -> p c d", d=D)
            iota = sb("iota", [P, P, UQ], BF16)
            hmask = sb("hmask", [P, 2], F32)
            left = [sb(f"left{n}", [P, P, UQ], BF16) for n in range(2)]
            onehot = sb("onehot", [P, LO, UQ], F16)
            right = [sb(f"right{n}", [P, 2, LO, 2, UQ], F16) for n in range(2)]
            tb = sb("tb", [P, W, 3, NC], F32)
            ids = sb("ids", [P, 2, W, NC], BF16)
            part = sb("part", [P, 2, W, NC], F16)
            wpart = sb("wpart", [P, 2, 2, W, NC], F16)
            zb = sb("zb", [P, 2, KD, BLK], F32R)
            yb = sb("yb", [P, W, D], F32)
            res = sb("res", [P, W, D], F32)

            dps = [ps(f"dps{n}", [P, 2, BLK]) for n in range(2)]
            cps = [ps(f"cps{n}", [P, PC, LO, 2]) for n in range(3)]
            ups = [ps(f"ups{n}", [P, BANK]) for n in range(2)]

            d_down = sem("d_down")
            c_iotab = sem("c_iotab")
            dt_ps = sem("dt_ps")
            dt_hi = sem("dt_hi")
            dt_ev = sem("dt_ev")
            d_zb = sem("d_zb")
            d_tb = sem("d_tb")
            d_yb = [sem(f"d_yb{w}") for w in range(W)]
            st_out = [sem(f"st_out{w}") for w in range(W)]
            p_ids = sem("p_ids")
            p_step = sem("p_step")
            p_w = sem("p_w")
            u_left = sem("u_left")
            u_one = sem("u_one")
            u_ready = sem("u_ready")
            down_done = sem("down_done")
            gelu_done = sem("gelu_done")
            c_done = sem("c_done")
            mul_done = sem("mul_done")
            up_done = [sem(f"up_done{w}") for w in range(W)]
            add_done = [sem(f"add_done{w}") for w in range(W)]

            def slots(par):
                return g[:, 0:2 + par:1 + par]

            block = ctx.enter_context(nc.Block())

            @block.sync
            def _(sp):
                sp.dma_start(down_raw, expert_down.rearrange("(p c) d -> p c d", c=LO)).then_inc(d_down, 16)

                def body(i, first):
                    if not first:
                        sp.wait_ge(p_w, i)
                    for w in range(W):
                        sp.dma_start(tb[:, w].rearrange("p a q -> p (a q)"),
                                     tab_scratch[W * i + W + w]).then_inc(d_tb, 16)
                    if not first:
                        sp.wait_ge(down_done, ND2 * i)
                    sp.dma_start(zb[:].rearrange("p a k t -> p (a k t)").bitcast(F32), z_scratch[i]).then_inc(d_zb, 16)
                    if not first:
                        store(i - 1, 0)
                    load_y(i, 0)
                    if not first:
                        store(i - 1, 1)
                    load_y(i, 1)

                def load_y(i, w):
                    sp.dma_start(yb[:, w], out_blk[i, :, w]).then_inc(d_yb[w], 16)

                def store(i, w):
                    sp.wait_ge(add_done[w], i + 1)
                    sp.dma_start(out_blk[i, :, w], res[:, w]).then_inc(st_out[w], 16)

                body(0, True)
                with sp.Fori(1, NI) as i:
                    body(i, False)
                for w in range(W):
                    store(NI - 1, w)
                for w in range(W):
                    sp.wait_ge(st_out[w], 16 * NI)

            @block.gpsimd
            def _(pool):
                pool.iota(iota[:], pattern=[[1, P], [0, UQ]], base=0, channel_multiplier=0,
                          allow_small_or_imprecise_dtypes=True).then_inc(c_iotab, 1)
                pool.memset(hmask[:], 1.0).then_inc(c_iotab, 1)
                pool.wait_ge(c_iotab, 2)
                pool.affine_select(out=hmask[:, 0:1], in_=hmask[:, 0:1], compare_op=ALU.is_ge, fill=0.0, base=63,
                                   pattern=[[0, 1]], channel_multiplier=-1).then_inc(c_iotab, 1)
                pool.affine_select(out=hmask[:, 1:2], in_=hmask[:, 1:2], compare_op=ALU.is_ge, fill=0.0, base=-64,
                                   pattern=[[0, 1]], channel_multiplier=1).then_inc(c_iotab, 1)

            @block.scalar
            def _(act):
                act.preload_act_table(ACT.Gelu)
                for u in range(LO * KD // 4):
                    k, c0 = u % KD, 4 * (u // KD)
                    act.wait_ge(dt_ps, u + 1)
                    act.activation(wd_h[:, c0:c0 + 4, k], dps[u % 2][:].rearrange("p a t -> p (a t)").rearrange(
                        "p (c e) -> p c e", c=4), ACT.Copy, scale=nrm[:, k:k + 1]).then_inc(dt_hi, 1)

                def body(i, par):
                    for m in range(ND2):
                        act.wait_ge(down_done, ND2 * i + m + 1)
                        act.activation(slots(par)[:, :, 2 * m:2 * m + 2].rearrange("p w c t -> p c w t"),
                                       dps[m % 2][:].rearrange("p c (w t) -> p c w t", w=W),
                                       ACT.Gelu).then_inc(gelu_done, 1)

                for i in range(2):
                    body(i, i)
                with act.Fori(1, NI // 2) as j:
                    for par in range(2):
                        body(2 * j + par, par)

            @block.vector
            def _(dve):
                for u in range(LO * KD // 4):
                    k = u % KD
                    c0 = 4 * (u // KD)
                    src = dps[u % 2][:].rearrange("p a t -> p (a t)").rearrange("p (c e) -> p c e", c=4)
                    dve.wait_ge(dt_hi, u + 1)
                    dve.scalar_tensor_tensor(out=wd_l[:, c0:c0 + 4, k], in0=src, scalar=nrm[:, k:k + 1],
                                             in1=wd_h[:, c0:c0 + 4, k].bitcast(F32), op0=ALU.mult,
                                             op1=ALU.subtract).then_inc(dt_ev, 1)
                dve.wait_ge(c_iotab, 4)

                def prepare(i, first):
                    b = 2 * i
                    dve.wait_ge(d_tb, 16 * W * i + 16 * W)
                    if not first:
                        dve.wait_ge(u_ready, NUN * i)
                    for a in range(2):
                        last = dve.tensor_copy(ids[:, a], tb[:, :, a])
                    last.then_inc(p_ids, 1)
                    wt = tb[:, :, 2]
                    dve.tensor_copy(part[:, 0], wt).then_inc(p_step, 1)
                    dve.wait_ge(p_step, b + 1)
                    dve.tensor_tensor(out=part[:, 1], in0=wt, in1=part[:, 0], op=ALU.subtract).then_inc(p_step, 1)
                    dve.wait_ge(p_step, b + 2)
                    for half in range(2):
                        last = dve.tensor_scalar(out=wpart[:, :, half], in0=part[:], scalar1=hmask[:, half:half + 1],
                                                 scalar2=None, op0=ALU.mult)
                    last.then_inc(p_w, 1)

                def build(i, u, first):
                    w, q0 = u // 2, (u % 2) * UQ

                    def left_rows():
                        if u == 0:
                            dve.wait_ge(p_ids, i + 1)
                            dve.wait_ge(p_w, i + 1)
                        if u >= 2 or not first:
                            dve.wait_ge(c_done, NP * i + 4 * u - 4)
                        dve.tensor_tensor(out=left[u % 2][:],
                                          in0=ids[:, 0, w, q0:q0 + UQ].unsqueeze(1).broadcast_to([P, P, UQ]),
                                          in1=iota[:], op=ALU.is_equal)

                    def onehot_rows():
                        if u > 0:
                            dve.wait_ge(u_ready, NUN * i + u)
                        dve.tensor_tensor(out=onehot[:],
                                          in0=ids[:, 1, w, q0:q0 + UQ].unsqueeze(1).broadcast_to([P, LO, UQ]),
                                          in1=iota[:, 0:LO], op=ALU.is_equal).then_inc(u_one, 1)

                    def right_rows(s):
                        dve.wait_ge(u_one, NUN * i + u + 1)
                        ins = dve.tensor_tensor(
                            out=right[u % 2][:, s], in0=onehot[:].unsqueeze(2).broadcast_to([P, LO, 2, UQ]),
                            in1=wpart[:, s, :, w, q0:q0 + UQ].unsqueeze(1).broadcast_to([P, LO, 2, UQ]), op=ALU.mult)
                        if s == 1:
                            ins.then_inc(u_ready, 1)

                    return [left_rows, onehot_rows, lambda: right_rows(0), lambda: right_rows(1)]

                def times_c(i, par, n):
                    w, q0 = n // 8, (n % 8) * PC
                    if n == 0:
                        dve.wait_ge(gelu_done, ND2 * i + ND2)
                    dve.wait_ge(c_done, NP * i + n + 1)
                    tok = slots(par)[:, w].rearrange("p c (e q) -> p c e q", e=2)
                    for half in range(2):
                        gv = tok[:, :, half, q0:q0 + PC]
                        last = dve.tensor_tensor(out=gv, in0=cps[n % 3][:, :, :, half].rearrange("p q c -> p c q"),
                                                 in1=gv, op=ALU.mult)
                    last.then_inc(mul_done, 1)

                def finish(i, w, first):
                    dve.wait_ge(d_yb[w], 16 * i + 16)
                    if not first:
                        dve.wait_ge(st_out[w], 16 * i)
                    dve.wait_ge(up_done[w], i + 1)
                    dve.scalar_tensor_tensor(out=res[:, w], in0=ups[w][:, 0:D], scalar=unscale[:, bass.ds(W * i + w, 1)],
                                             in1=yb[:, w], op0=ALU.mult, op1=ALU.add).then_inc(add_done[w], 1)

                def body(i, par, first):
                    prepare(i, first)
                    for step in build(i, 0, first) + build(i, 1, first):
                        step()
                    steps = {}
                    for u in range(2, NUN):
                        for m, step in enumerate(build(i, u, first)):
                            steps[4 * u - 5 + m] = step
                    for n in range(NP):
                        times_c(i, par, n)
                        if n in steps:
                            steps[n]()
                        if n == 9 and not first:
                            finish(i - 1, 1, isinstance(i, int) and i == 1)
                    finish(i, 0, first)

                for i in range(2):
                    body(i, i, i == 0)
                with dve.Fori(1, NI // 2) as j:
                    for par in range(2):
                        body(2 * j + par, par, False)
                finish(NI - 1, 1, False)

            @block.tensor
            def _(pe):
                pe.wait_ge(d_down, 16)
                for u in range(LO * KD // 4):
                    k = u % KD
                    c0 = 4 * (u // KD)
                    dst = dps[u % 2][:].rearrange("p a t -> p (a t)")
                    if u >= 2:
                        pe.wait_ge(dt_ev, u - 1)
                    for c in range(4):
                        last = pe.transpose(dst[:, c * P:(c + 1) * P], down_raw[:, c0 + c, k * P:(k + 1) * P], ident[:])
                    last.then_inc(dt_ps, 1)
                pe.wait_ge(dt_ev, LO * KD // 4)

                def c_piece(i, n, first):
                    if n % 4 == 0:
                        pe.wait_ge(u_ready, NUN * i + n // 4 + 1)
                    if n >= 3 or not first:
                        pe.wait_ge(mul_done, NP * i + n - 2)
                    u, pc = n // 4, n % 4
                    for q in range(PC):
                        for s in range(2):
                            last = pe.matmul(cps[n % 3][:, q], left[u % 2][:, :, pc * PC + q],
                                             right[u % 2][:, s, :, :, pc * PC + q],
                                             start=(s == 0), stop=(s == 1))
                    last.then_inc(c_done, 1)

                def up(i, par, w, c0, n, first):
                    if c0 == 0:
                        pe.wait_ge(mul_done, NP * i + 8 * w + 8)
                        if not first:
                            pe.wait_ge(add_done[w], i)
                    for c in range(c0, c0 + n):
                        last = pe.matmul(ups[w][:, 0:D], slots(par)[:, w, c], upw[:, c],
                                         start=(c == 0), stop=(c == LO - 1))
                    if c0 + n == LO:
                        last.then_inc(up_done[w], 1)

                def body(i, par, first):
                    pe.wait_ge(d_zb, 16 * i + 16)
                    for m in range(ND2):
                        if m >= 2 or not first:
                            pe.wait_ge(gelu_done, ND2 * i + m - 1)
                        for c in range(2):
                            for k in range(KD):
                                last = split3(pe, dps[m % 2][:, c], wd_h[:, 2 * m + c, k], wd_l[:, 2 * m + c, k],
                                              zb[:, 0, k], zb[:, 1, k], k == 0, k == KD - 1)
                        last.then_inc(down_done, 1)
                    for n in range(8):
                        c_piece(i, n, first)
                        if not first:
                            up(i - 1, 1 - par, 1, 4 * n, 4, isinstance(i, int) and i == 1)
                    c_piece(i, 8, first)
                    for n in range(8):
                        up(i, par, 0, 4 * n, 4, first)
                        if n < 7:
                            c_piece(i, 9 + n, first)

                for i in range(2):
                    body(i, i, i == 0)
                with pe.Fori(1, NI // 2) as j:
                    for par in range(2):
                        body(2 * j + par, par, False)
                up(NI - 1, 1, 1, 0, LO, False)


_INS = ['L0_attn_x', 'L0_attn_gamma', 'L0_attn_w_qkv', 'L0_attn_w_out', 'L0_attn_pm_k', 'L0_attn_pm_v',
        'L0_ffn_w_q', 'L0_ffn_keys', 'L0_ffn_expert_down', 'L0_ffn_expert_up', 'L0_ffn_norm_w']


def kernel(**inputs):
    import numpy as np
    import concourse.bacc as bacc
    from concourse.bass_utils import run_bass_kernel_spmd

    nc = bacc.Bacc("TRN2", target_bir_lowering=False, num_devices=1)
    arrays, args = {}, []
    for name in _INS:
        a = np.ascontiguousarray(inputs[name])
        arrays[f"in_{name}"] = a
        args.append(nc.dram_tensor(f"in_{name}", a.shape, mybir.dt.from_np(a.dtype), kind="ExternalInput").ap())
    shape = arrays['in_L0_attn_x'].shape
    args.append(nc.dram_tensor("out_0", shape, F32, kind="ExternalOutput").ap())
    attention_experts(nc, *args)
    r = run_bass_kernel_spmd(nc, [arrays], core_ids=[0])
    return r.results[0]["out_0"]
```

```python
from contextlib import ExitStack

import concourse.bass as bass
from concourse import mybir

ALU = mybir.AluOpType
ACT = mybir.ActivationFunctionType
AX = mybir.AxisListType
F32 = mybir.dt.float32
F32R = mybir.dt.float32r
BF16 = mybir.dt.bfloat16
F16 = mybir.dt.float16
U32 = mybir.dt.uint32

P = 128
BANK = 512
SEG = 128
W = 2
BLK = W * SEG
TOP = 8


def attention_experts(nc, x, gamma, w_qkv, w_out, pm_k, pm_v, w_q, keys, expert_down, expert_up, norm_w, out):
    B, S, D = x.shape
    HEADS, PM, DH = pm_k.shape
    EH, NK, _, DK = keys.shape
    INNER = HEADS * DH
    NEXP = expert_down.shape[0]
    KD = D // P
    NI = B * S // BLK
    CH = INNER // P
    KJ = PM + SEG
    NG = W * HEADS // 4
    HS = EH * 2
    NC = EH * TOP
    LO = NEXP // P
    assert D == 256 and DH == 64 and HEADS == 16 and KJ * 2 <= BANK and NC == 64 and LO == 32 and NK == 64
    assert DK == P and PM * 8 == P
    ROOT = float(DH) ** -0.5

    x_blk = x.rearrange("b s d -> (b s) d").rearrange("(n w p) d -> n p w d", w=W, p=P)
    out_blk = out.rearrange("b s d -> (b s) d").rearrange("(n w p) d -> n p w d", w=W, p=P)
    z_scratch = nc.dram_tensor("z_scratch", [NI, P, 2 * KD * BLK], F32, kind="Internal").ap()
    tab_scratch = nc.dram_tensor("tab_scratch", [W * (NI + 1), P, 3 * 64], F32, kind="Internal").ap()

    with ExitStack() as whole:
        def sem(name):
            return whole.enter_context(nc.semaphore(name))

        def shared(name, shape, dt):
            return whole.enter_context(nc.sbuf_tensor(name, shape, dt))

        ident = shared("ident", [P, P], F32)
        identb = shared("identb", [P, P], BF16)
        gam = shared("gam", [P, KD], F32)
        nrm = shared("nrm", [P, KD], F32)
        with ExitStack() as place:
            raw = place.enter_context(nc.sbuf_tensor("raw", [P, LO * D], F32))
        with ExitStack() as place:
            wout_h, wout_l, pmv_h, pmv_l, oT_l, pmT_l = (
                place.enter_context(nc.sbuf_tensor(name, shape, F32R)) for name, shape in (
                    ("wout_h", [P, CH, D]), ("wout_l", [P, CH, D]), ("pmv_h", [P, 2, 8 * DH]),
                    ("pmv_l", [P, 2, 8 * DH]), ("oT_l", [P, CH, P]), ("pmT_l", [P, 2, P])))
        upw = shared("upw", [P, LO, D], F32)
        unscale = shared("unscale", [P, W * NI], F32)
        with ExitStack() as place:
            wqkv_h, wqkv_l = (place.enter_context(nc.sbuf_tensor(f"wqkv_{part}", [P, KD, 3 * INNER], F32R))
                              for part in ("h", "l"))
        early = shared("early", [P, 3 * LO * P], F32)
        down_raw = early[:, 0:LO * D].rearrange("p (c d) -> p c d", d=D)

        c_ident = sem("c_ident")
        c_mask = sem("c_mask")
        c_iota = sem("c_iota")
        d_small = sem("d_small")
        d_down = sem("d_down")
        d_up = sem("d_up")

        with ExitStack() as ctx:
            def sb(name, shape, dt):
                return ctx.enter_context(nc.sbuf_tensor(name, shape, dt))

            def ps(name, shape, dt=F32):
                return ctx.enter_context(nc.psum_tensor(name, shape, dt))

            maskneg = sb("maskneg", [P, KJ], BF16)
            iota8 = sb("iota8", [P, TOP], F32)
            minus_half = sb("minus_half", [P, W], F32)
            eps = sb("eps", [P, 2, W], F32)
            one = sb("one", [P, 1], F32)
            blank = sb("blank", [P, 2], F32)
            assert 3 * LO * P == 2 * KD * 3 * INNER
            wsc_h = sb("wsc_h", [P, KD, HS * NK], F32R)
            wsc_l = sb("wsc_l", [P, KD, HS * NK], F32R)
            wout = sb("wout", [P, CH, D], F32)
            pmk2 = sb("pmk2", [P, 2, 2 * DH], F32)
            pmv_bd = sb("pmv_bd", [P, 2, 8 * DH], F32)
            xin = sb("xin", [P, W, D], F32)
            xres = sb("xres", [P, W, D], F32)
            stats = sb("stats", [P, W, 6], F32)
            mv = sb("mv", [P, W, 2], F32)
            rr = sb("rr", [P, 6, W], F32)
            z = sb("z", [P, W, D], F32)
            zhl = sb("zhl", [P, 2, KD, BLK], F32R)
            qT = sb("qT", [P, CH, BLK], F32)
            kT = sb("kT", [P, CH, W, KJ], F32)
            v = sb("v", [P, W, INNER], F32)
            sc = sb("sc", [P, W, HS * NK], F32)
            prob = [sb(f"prob{n}", [P, 8, KJ], F32) for n in range(2)]
            probT = [sb(f"probT{n}", [P, 4, P], F32) for n in range(2)]
            probpm = sb("probpm", [P, 2, 8, PM], F32)
            pmT_h = sb("pmT_h", [P, 2, P], F32R)
            negmax = sb("negmax", [P, NG, 2, 2], F32)
            rowsum = sb("rowsum", [P, NG, 4], F32)
            recip = sb("recip", [P, 8], F32)
            o = sb("o", [P, INNER], F32)
            oT_h = sb("oT_h", [P, CH, P], F32R)
            y = sb("y", [P, W, D], F32)
            top = sb("top", [P, HS, TOP], F32)
            topi = sb("topi", [P, HS, TOP], U32)
            topf = sb("topf", [P, HS, TOP], F32)
            cand = sb("cand", [P, EH, TOP, TOP], F32)
            best = sb("best", [P, NC], F32)
            besti = sb("besti", [P, NC], U32)
            rank = sb("rank", [P, 2, NC], U32)
            pick = sb("pick", [P, NC, TOP], F32)
            prod = sb("prod", [P, NC, TOP], F32)
            big = sb("big", [P, 5], F32)
            spare = sb("spare", [P, 1], F32)
            keyi = sb("keyi", [P, 2, NC], F32)
            high = sb("high", [P, NC], F32)
            tab = sb("tab", [P, W, 3, 2, NC], F32)
            tabT = sb("tabT", [P, W, 3, NC], F32)

            aux = [ps(f"aux{n}", [P, BANK]) for n in range(2)]
            sim = [ps(f"sim{n}", [P, 2, BANK]) for n in range(2)]
            ptb = ps("ptb", [P, 4, P])
            pvb = ps("pvb", [P, BANK])

            d_raw = [sem(f"d_raw{k}") for k in range(KD)]
            d_wq = sem("d_wq")
            d_pmv = sem("d_pmv")
            d_wout = sem("d_wout")
            c_pmv0 = sem("c_pmv0")
            c_roots = sem("c_roots")
            set_ps = sem("set_ps")
            set_ev = sem("set_ev")
            w_hi = sem("w_hi")
            wqkv_hi = sem("wqkv_hi")
            w_split = sem("w_split")
            d_xin = sem("d_xin")
            d_xres = sem("d_xres")
            st_z = sem("st_z")
            st_tab = [sem(f"st_tab{w}") for w in range(W)]
            st_y = [sem(f"st_y{w}") for w in range(W)]
            ln_bn = sem("ln_bn")
            ln_mv = sem("ln_mv")
            ln_step = sem("ln_step")
            ln_r = sem("ln_r")
            z_ready = sem("z_ready")
            z_hi = sem("z_hi")
            aux_full = sem("aux_full")
            aux_act = sem("aux_act")
            aux_dve = sem("aux_dve")
            qk_done = sem("qk_done")
            max_done = sem("max_done")
            exp_done = sem("exp_done")
            pm_packed = sem("pm_packed")
            pt_done = sem("pt_done")
            pt_ev = sem("pt_ev")
            pv_done = sem("pv_done")
            rcp = sem("rcp")
            norm_done = sem("norm_done")
            late_full = sem("late_full")
            oT_hi = sem("oT_hi")
            late_lo = sem("late_lo")
            pm_hi = sem("pm_hi")
            split_hi = sem("split_hi")
            split_lo = sem("split_lo")
            t_top = sem("t_top")
            t_topi = sem("t_topi")
            t_topf = sem("t_topf")
            t_cand = sem("t_cand")
            t_best = sem("t_best")
            t_scale = sem("t_scale")
            t_inv = sem("t_inv")
            t_besti = sem("t_besti")
            t_rank = sem("t_rank")
            t_pick = sem("t_pick")
            t_prod = sem("t_prod")
            t_key = sem("t_key")
            t_high = sem("t_high")
            tab_ready = sem("tab_ready")

            USES = ([(f"qk{m}", "A") for m in range(4)] + [("wo1", "D")]
                    + [(f"qk{m}", "A") for m in range(4, 8)] + [(f"v{m}", "A") for m in range(4)]
                    + [("tab0", "D"), ("pm0", "D"), ("sc0", "A"), ("sc1", "A"), ("pm1", "D"), ("sc2", "A"),
                       ("sc3", "A"), ("tab1", "D"), ("pm2", "D"), ("oT0", "D"), ("oT1", "D"), ("zT0", "D"), ("zT1", "D"),
                       ("pm3", "D"), ("wo0", "D")])
            NU = len(USES)
            UI = {name: n for n, (name, _) in enumerate(USES)}
            NA = sum(e == "A" for _, e in USES)
            ND = NU - NA
            assert NU % 2 == 0

            def emptied(name):
                u = UI[name]
                who = USES[u][1]
                return who, sum(e == who for _, e in USES[:u + 1])

            def wait_emptied(eng, i, name):
                who, n = emptied(name)
                eng.wait_ge(aux_act if who == "A" else aux_dve, i * (NA if who == "A" else ND) + n)

            def bank(name):
                return aux[UI[name] % 2]

            def split3(pe, outp, wh, wl, xh, xl, first, last):
                pe.matmul(outp, wl, xh, start=first, stop=False)
                pe.matmul(outp, wh, xl, start=False, stop=False)
                return pe.matmul(outp, wh, xh, start=False, stop=last)

            block = ctx.enter_context(nc.Block())

            @block.sync
            def _(sp):
                sp.dma_start(xin[:], x_blk[0]).then_inc(d_xin, 16)
                sp.dma_start(gam[:], gamma.rearrange("(k p) -> p k", p=P), allow_slow_non_contiguous=True).then_inc(d_small, 16)
                sp.dma_start(nrm[:], norm_w.rearrange("(k p) -> p k", p=P), allow_slow_non_contiguous=True).then_inc(d_small, 16)
                pmk_rows = pm_k.rearrange("(a h) p d -> (h p) a d", a=2)
                for copy in range(2):
                    sp.dma_start(pmk2[:, :, copy * DH:(copy + 1) * DH], pmk_rows).then_inc(d_small, 16)
                for k in range(KD):
                    sp.dma_start(raw[:, k * 3 * INNER:(k + 1) * 3 * INNER], w_qkv[k * P:(k + 1) * P]).then_inc(d_raw[k], 16)
                sp.dma_start(raw[0:NK, KD * 3 * INNER:].rearrange("p (h n) -> p h n", h=EH),
                             keys.rearrange("h k s d -> k h (s d)")).then_inc(d_wq, 16)
                wq_rows = w_q.rearrange("(m p) d -> p m d", p=P)
                sp.dma_start(v[:].rearrange("p w (m d) -> p (w m) d", d=D), wq_rows[:, 0:8]).then_inc(d_wq, 16)
                sp.dma_start(sc[:].rearrange("p w (m d) -> p (w m) d", d=D), wq_rows[:, 8:16]).then_inc(d_wq, 16)
                sp.dma_start(wout[:], w_out.rearrange("(c p) n -> p c n", p=P)).then_inc(d_wout, 16)
                sp.wait_ge(c_pmv0, 1)
                for hh in range(8):
                    sp.dma_start(pmv_bd[hh * PM:(hh + 1) * PM, :, hh * DH:(hh + 1) * DH],
                                 pm_v.rearrange("(a h) p d -> h p a d", a=2)[hh]).then_inc(d_pmv, 16)

                def store_z(i):
                    sp.dma_start(z_scratch[i], zhl[:].rearrange("p a k t -> p (a k t)").bitcast(F32)).then_inc(st_z, 16)

                def body(i, first, last):
                    sp.wait_ge(z_ready, W * i + W)
                    sp.dma_start(xin[:], x_blk[NI - 1 if last else i + 1]).then_inc(d_xin, 16)
                    if not first:
                        wait_emptied(sp, i, "wo1")
                        sp.dma_start(out_blk[i - 1, :, 1], y[:, 1]).then_inc(st_y[1], 16)
                    sp.dma_start(xres[:], x_blk[i]).then_inc(d_xres, 16)
                    if last:
                        sp.wait_ge(aux_full, NU * i + UI["v3"] + 1)
                        sp.dma_start(down_raw, expert_down.rearrange("(p c) d -> p c d", c=LO)).then_inc(d_down, 16)
                    wait_emptied(sp, i, "tab0")
                    sp.dma_start(tab_scratch[W * i], tabT[:, 0].rearrange("p a q -> p (a q)")).then_inc(st_tab[0], 16)
                    wait_emptied(sp, i, "tab1")
                    sp.dma_start(tab_scratch[W * i + 1], tabT[:, 1].rearrange("p a q -> p (a q)")).then_inc(st_tab[1], 16)
                    if not last:
                        wait_emptied(sp, i, "zT1")
                        store_z(i + 1)
                    wait_emptied(sp, i, "wo0")
                    sp.dma_start(out_blk[i, :, 0], y[:, 0]).then_inc(st_y[0], 16)

                sp.wait_ge(set_ev, 9)
                store_z(0)
                body(0, True, False)
                with sp.Fori(1, NI - 1) as i:
                    body(i, False, False)
                body(NI - 1, False, True)
                sp.wait_ge(aux_dve, NI * ND + 1)
                sp.dma_start(out_blk[NI - 1, :, 1], y[:, 1]).then_inc(st_y[1], 16)
                for w in range(W):
                    sp.wait_ge(aux_dve, NI * ND + w + 2)
                    sp.dma_start(tab_scratch[W * NI + w], tabT[:, w].rearrange("p a q -> p (a q)")).then_inc(st_tab[w], 16)
                sp.wait_ge(st_z, 16 * NI)
                for w in range(W):
                    sp.wait_ge(st_tab[w], 16 * (NI + 1))
                    sp.wait_ge(st_y[w], 16 * (NI + w))
                sp.wait_ge(d_small, 16 * 4)

            @block.gpsimd
            def _(pool):
                pool.memset(ident[:], 0.0).then_inc(c_ident, 1)
                pool.wait_ge(c_ident, 1)
                pool.affine_select(out=ident[:], in_=ident[:], compare_op=ALU.not_equal, fill=1.0, base=0,
                                   pattern=[[-1, P]], channel_multiplier=1).then_inc(c_ident, 1)
                pool.memset(minus_half[:], -0.5).then_inc(c_roots, 1)
                pool.memset(eps[:, 0], 1e-5).then_inc(c_roots, 1)
                pool.memset(eps[:, 1], 1e-6).then_inc(c_roots, 1)
                pool.memset(one[:], 1.0).then_inc(c_roots, 1)
                pool.memset(blank[:, 0:1], 0.0).then_inc(aux_dve, 1)
                pool.memset(blank[:, 1:2], 0.0).then_inc(st_y[1], 16)
                pool.memset(pmv_bd[:], 0.0).then_inc(c_pmv0, 1)
                for w in range(W):
                    pool.memset(tab[:, w], 0.0).then_inc(tab_ready, 1)
                pool.memset(identb[:], 0.0).then_inc(c_mask, 1)
                pool.memset(maskneg[:], 0.0).then_inc(c_mask, 1)
                pool.wait_ge(c_mask, 2)
                pool.affine_select(out=identb[:], in_=identb[:], compare_op=ALU.not_equal, fill=1.0, base=0,
                                   pattern=[[-1, P]], channel_multiplier=1).then_inc(c_mask, 1)
                pool.affine_select(out=maskneg[:, PM:KJ], in_=maskneg[:, PM:KJ], compare_op=ALU.is_ge, fill=-1e37,
                                   base=0, pattern=[[-1, SEG]], channel_multiplier=1).then_inc(c_mask, 1)
                pool.iota(iota8[:], pattern=[[1, TOP]], base=0, channel_multiplier=0,
                          allow_small_or_imprecise_dtypes=True).then_inc(c_iota, 1)

                def roots(i):
                    b = 6 * i
                    pool.wait_ge(ln_mv, W * i + W)
                    pool.tensor_tensor(out=rr[:, 0], in0=mv[:, :, 1], in1=eps[:, 0], op=ALU.add).then_inc(ln_step, 1)
                    pool.wait_ge(ln_step, b + 1)
                    pool.tensor_tensor(out=rr[:, 1], in0=rr[:, 0], in1=minus_half[:], op=ALU.pow).then_inc(ln_step, 1)
                    pool.wait_ge(ln_step, b + 2)
                    pool.tensor_tensor(out=rr[:, 2], in0=rr[:, 1], in1=rr[:, 1], op=ALU.mult).then_inc(ln_step, 1)
                    pool.wait_ge(ln_step, b + 3)
                    pool.tensor_tensor(out=rr[:, 3], in0=rr[:, 2], in1=mv[:, :, 1], op=ALU.mult).then_inc(ln_step, 1)
                    pool.wait_ge(ln_step, b + 4)
                    pool.tensor_tensor(out=rr[:, 2], in0=rr[:, 3], in1=eps[:, 1], op=ALU.add).then_inc(ln_step, 1)
                    pool.wait_ge(ln_step, b + 5)
                    pool.tensor_tensor(out=rr[:, 4], in0=rr[:, 2], in1=minus_half[:], op=ALU.pow).then_inc(ln_step, 1)
                    pool.wait_ge(ln_step, b + 6)
                    pool.tensor_tensor(out=rr[:, 5], in0=rr[:, 4], in1=rr[:, 1], op=ALU.mult).then_inc(ln_r, 1)

                def body(i):
                    for half in range(4):
                        if half == 2:
                            roots(i + 1)
                        pool.wait_ge(exp_done, NG * i + 2 * half + 2)
                        if half >= 2:
                            pool.wait_ge(aux_full, NU * i + UI[f"pm{half - 2}"] + 1)
                        pool.tensor_tensor(out=probpm[:, half % 2], in0=prob[half % 2][:, :, 0:PM],
                                           in1=one[:].unsqueeze(2).broadcast_to([P, 8, PM]),
                                           op=ALU.mult).then_inc(pm_packed, 1)

                pool.wait_ge(c_roots, 4)
                roots(0)
                body(0)
                with pool.Fori(1, NI) as i:
                    body(i)

            @block.scalar
            def _(act):
                act.preload_act_table(ACT.Exp)
                act.wait_ge(d_small, 16 * 4)
                for k in range(KD):
                    act.wait_ge(d_raw[k], 16)
                    act.activation(wqkv_h[:, k], raw[:, k * 3 * INNER:(k + 1) * 3 * INNER], ACT.Copy,
                                   scale=gam[:, k:k + 1]).then_inc(wqkv_hi, 1)

                act.wait_ge(w_split, KD)
                act.wait_ge(set_ps, 3)
                act.wait_ge(d_wout, 16)
                act.activation(wout_h[:], wout[:], ACT.Copy).then_inc(split_hi, 1)
                act.wait_ge(d_pmv, 16 * 8)
                act.activation(pmv_h[:], pmv_bd[:], ACT.Copy).then_inc(split_hi, 1)

                def empty(i, name, outp, inp, scale=1.0):
                    act.wait_ge(aux_full, NU * i + UI[name] + 1)
                    act.activation(outp, inp, ACT.Copy, scale=scale).then_inc(aux_act, 1)

                def oT_half(m):
                    return oT_h[:, 4 * (m % 2):4 * (m % 2) + 4, :]

                def late_hi(i, m):
                    act.wait_ge(late_full, 2 * i - 1 + m)
                    act.activation(oT_half(m), ptb[:], ACT.Copy).then_inc(oT_hi, 1)

                def body(i, first):
                    if not first:
                        late_hi(i, 0)
                    for m in range(4):
                        empty(i, f"qk{m}", qT[:, 2 * m:2 * m + 2, :],
                              bank(f"qk{m}")[:].rearrange("p (c t) -> p c t", c=2), scale=ROOT)
                        if m == 1 and not first:
                            late_hi(i, 1)
                    for m in range(4):
                        empty(i, f"qk{4 + m}", kT[:, 2 * m:2 * m + 2, :, PM:KJ],
                              bank(f"qk{4 + m}")[:].rearrange("p (c w t) -> p c w t", c=2, w=W))

                    def empty_v(m):
                        empty(i, f"v{m}", v[:, m // 2, (m % 2) * BANK:(m % 2 + 1) * BANK], bank(f"v{m}")[:])

                    empty_v(0)
                    empty_v(1)

                    def empty_sc(m):
                        if m % 2 == 0 and not first:
                            act.wait_ge(t_topi, W * i + m // 2 - 1)
                        empty(i, f"sc{m}", sc[:, m // 2, (m % 2) * BANK:(m % 2 + 1) * BANK], bank(f"sc{m}")[:])

                    def exps(n):
                        act.wait_ge(max_done, NG * i + n + 1)
                        if n % 2 == 0 and (n >= 4 or not first):
                            act.wait_ge(pm_packed, 4 * i + n // 2 - 1)
                        for j in range(2):
                            for par in range(2):
                                slot = 4 * (n % 2) + 2 * j + par
                                last = act.activation(
                                    prob[n // 2 % 2][:, slot, :], sim[n % 2][:, par, j * KJ:(j + 1) * KJ], ACT.Exp,
                                    bias=negmax[:, n, par, j:j + 1], scale=1.0,
                                    accum_out=rowsum[:, n, 2 * j + par:2 * j + par + 1])
                        last.then_inc(exp_done, 1)

                    for n in range(NG):
                        if n != 1:
                            exps(n)
                        if n == 0:
                            empty_v(2)
                            exps(1)
                        elif 2 <= n < 6:
                            empty_sc(n - 2)
                        elif n == 6:
                            for m in range(2):
                                act.wait_ge(aux_full, NU * i + UI[f"oT{m}"] + 1)
                                act.activation(oT_half(m), bank(f"oT{m}")[:].rearrange("p (c t) -> p c t", c=4),
                                               ACT.Copy).then_inc(oT_hi, 1)
                        act.wait_ge(pt_done, NG * i + n + 1)
                        act.activation(probT[n % 2][:], ptb[:], ACT.Copy).then_inc(pt_ev, 1)
                        if n == 0:
                            empty_v(3)

                body(0, True)
                with act.Fori(1, NI) as i:
                    body(i, False)
                for m in range(2):
                    late_hi(NI, m)

            @block.vector
            def _(dve):
                WO1_AFTER = 5
                def setup():
                    dve.wait_ge(d_small, 16 * 4)
                    for k in range(KD):
                        rw = raw[:, k * 3 * INNER:(k + 1) * 3 * INNER]
                        dve.wait_ge(wqkv_hi, k + 1)
                        dve.scalar_tensor_tensor(out=wqkv_l[:, k], in0=rw, scalar=gam[:, k:k + 1],
                                                 in1=wqkv_h[:, k].bitcast(F32), op0=ALU.mult,
                                                 op1=ALU.subtract).then_inc(w_split, 1)
                    dve.wait_ge(set_ps, 1)
                    for half in range(2):
                        rows = aux[0][:, half * P:(half + 1) * P].rearrange("p (c e s) -> p c e s", e=2, s=PM)
                        for par in range(2):
                            for w in range(W):
                                last = dve.tensor_copy(kT[par * DH:(par + 1) * DH, 4 * half:4 * half + 4, w, 0:PM],
                                                       rows[par * DH:(par + 1) * DH, :, par, :])
                    last.then_inc(set_ev, 1)
                    for n in range(2):
                        dve.wait_ge(set_ps, 2 + n)
                        dve.tensor_copy(o[:, n * BANK:(n + 1) * BANK], aux[(1 + n) % 2][:]).then_inc(set_ev, 1)
                    for k in range(KD):
                        for n in range(2):
                            u = 3 + 2 * k + n
                            dve.wait_ge(set_ps, u + 1)
                            hi = wsc_h[:, k, n * BANK:(n + 1) * BANK]
                            dve.tensor_scalar(out=hi, in0=aux[u % 2][:], scalar1=nrm[:, k:k + 1], scalar2=None,
                                              op0=ALU.mult).then_inc(w_hi, 1)
                            dve.wait_ge(w_hi, 2 * k + n + 1)
                            dve.scalar_tensor_tensor(out=wsc_l[:, k, n * BANK:(n + 1) * BANK], in0=aux[u % 2][:],
                                                     scalar=nrm[:, k:k + 1], in1=hi.bitcast(F32), op0=ALU.mult,
                                                     op1=ALU.subtract).then_inc(set_ev, 1)

                def moments(i):
                    dve.wait_ge(d_xin, 16 * i + 16)
                    for w in range(W):
                        dve.bn_stats(stats[:, w], xin[:, w]).then_inc(ln_bn, 1)

                def aggregate():
                    for w in range(W):
                        dve.bn_aggr(mv[:, w], stats[:, w]).then_inc(ln_mv, 1)

                def normed(i, first=False):
                    dve.wait_ge(ln_r, i + 1)
                    dve.wait_ge(ln_mv, W * i + W)
                    for w in range(W):
                        dve.tensor_scalar(out=z[:, w], in0=xin[:, w], scalar1=mv[:, w, 0:1],
                                          scalar2=rr[:, 5, w:w + 1], op0=ALU.subtract,
                                          op1=ALU.mult).then_inc(z_ready, 1)

                def split_z(w, b, count, done):
                    src = b[:, 0:KD * P].rearrange("p (k t) -> p k t", k=KD)
                    hi = zhl[:, 0, :, w * P:(w + 1) * P]
                    dve.tensor_copy(hi, src).then_inc(z_hi, 1)
                    dve.wait_ge(z_hi, count)
                    dve.tensor_tensor(out=zhl[:, 1, :, w * P:(w + 1) * P], in0=src, in1=hi.bitcast(F32),
                                      op=ALU.subtract).then_inc(done, 1)

                def choose(t, w):
                    s3 = sc[:, w].rearrange("p (m k) -> p m k", k=NK)

                    def tops(m0):
                        for m in range(m0, m0 + 8):
                            last = dve.max(top[:, m], s3[:, m])
                        if m0 == 8:
                            last.then_inc(t_top, 1)

                    def pairs():
                        dve.wait_ge(t_top, t + 1)
                        a = top[:].rearrange("p (h s) k -> p h s k", s=2)
                        dve.tensor_tensor(
                            out=cand[:], in0=a[:, :, 0, :].unsqueeze(3).broadcast_to([P, EH, TOP, TOP]),
                            in1=a[:, :, 1, :].unsqueeze(2).broadcast_to([P, EH, TOP, TOP]),
                            op=ALU.add).then_inc(t_cand, 1)

                    def topis(m0):
                        for m in range(m0, m0 + 8):
                            last = dve.max_index(topi[:, m], top[:, m], s3[:, m])
                        if m0 == 8:
                            last.then_inc(t_topi, 1)

                    def bests():
                        dve.wait_ge(t_topi, t + 1)
                        dve.wait_ge(t_cand, t + 1)
                        dve.tensor_copy(topf[:], topi[:]).then_inc(t_topf, 1)
                        for h in range(EH):
                            last = dve.max(best[:, h * TOP:(h + 1) * TOP], cand[:, h].rearrange("p a b -> p (a b)"))
                        last.then_inc(t_best, 1)

                    def scale():
                        dve.wait_ge(t_best, t + 1)
                        dve.tensor_reduce(out=big[:, 0:1], in_=best[:], axis=AX.X, op=ALU.max).then_inc(t_scale, 1)
                        dve.wait_ge(t_scale, 4 * t + 1)
                        dve.tensor_scalar(out=big[:, 1:2], in0=big[:, 0:1], scalar1=2.0 ** -100, scalar2=None,
                                          op0=ALU.max).then_inc(t_scale, 1)
                        dve.wait_ge(t_scale, 4 * t + 2)
                        dve.tensor_scalar(out=big[:, 2:3].bitcast(U32), in0=big[:, 1:2].bitcast(U32),
                                          scalar1=0x7F800000, scalar2=None, op0=ALU.bitwise_and).then_inc(t_scale, 1)
                        dve.wait_ge(t_scale, 4 * t + 3)
                        dve.tensor_scalar(out=big[:, 3:4], in0=big[:, 2:3], scalar1=2.0 ** -14, scalar2=None,
                                          op0=ALU.mult).then_inc(t_scale, 1)
                        dve.wait_ge(t_scale, 4 * t + 4)
                        dve.tensor_copy(unscale[:, bass.ds(t, 1)], big[:, 3:4])
                        dve.reciprocal(big[:, 4:5], big[:, 3:4]).then_inc(t_inv, 1)

                    def twice(a):
                        return a.unsqueeze(1).broadcast_to([P, 2, NC])

                    def bestis():
                        dve.wait_ge(t_inv, t + 1)
                        dve.tensor_scalar(out=tab[:, w, 2], in0=twice(best[:]), scalar1=0.0, scalar2=big[:, 4:5],
                                          op0=ALU.max, op1=ALU.mult)
                        for h in range(EH):
                            last = dve.max_index(besti[:, h * TOP:(h + 1) * TOP], best[:, h * TOP:(h + 1) * TOP],
                                                 cand[:, h].rearrange("p a b -> p (a b)"))
                        last.then_inc(t_besti, 1)

                    def ranks():
                        dve.wait_ge(t_besti, t + 1)
                        dve.tensor_scalar(out=rank[:, 0], in0=besti[:], scalar1=3, scalar2=None,
                                          op0=ALU.logical_shift_right)
                        dve.tensor_scalar(out=rank[:, 1], in0=besti[:], scalar1=7, scalar2=None,
                                          op0=ALU.bitwise_and).then_inc(t_rank, 1)

                    def lookup(s):
                        if s == 1:
                            dve.wait_ge(t_key, 2 * t + 1)
                        if s == 0:
                            dve.wait_ge(t_rank, t + 1)
                            dve.wait_ge(t_topf, t + 1)
                        dve.tensor_tensor(out=pick[:], in0=rank[:, s].unsqueeze(2).broadcast_to([P, NC, TOP]),
                                          in1=iota8[:].unsqueeze(1).broadcast_to([P, NC, TOP]),
                                          op=ALU.is_equal).then_inc(t_pick, 1)
                        dve.wait_ge(t_pick, 2 * t + s + 1)
                        f = topf[:].rearrange("p (h s) k -> p h s k", s=2)[:, :, s, :]
                        dve.tensor_tensor(
                            out=prod[:].rearrange("p (h c) a -> p h c a", c=TOP),
                            in0=pick[:].rearrange("p (h c) a -> p h c a", c=TOP),
                            in1=f.unsqueeze(2).broadcast_to([P, EH, TOP, TOP]), op=ALU.mult).then_inc(t_prod, 1)
                        dve.wait_ge(t_prod, 2 * t + s + 1)
                        dve.tensor_reduce(out=keyi[:, s], in_=prod[:], axis=AX.X, op=ALU.add).then_inc(t_key, 1)

                    def table():
                        dve.wait_ge(t_key, 2 * t + 2)
                        dve.tensor_scalar(out=high[:], in0=keyi[:, 1], scalar1=float(LO), scalar2=None,
                                          op0=ALU.is_ge).then_inc(t_high, 1)
                        dve.wait_ge(t_high, t + 1)
                        dve.scalar_tensor_tensor(out=tab[:, w, 0], in0=twice(keyi[:, 0]), scalar=float(NK // LO),
                                                 in1=twice(high[:]), op0=ALU.mult, op1=ALU.add)
                        dve.scalar_tensor_tensor(out=tab[:, w, 1], in0=twice(high[:]), scalar=-float(LO),
                                                 in1=twice(keyi[:, 1]), op0=ALU.mult,
                                                 op1=ALU.add).then_inc(tab_ready, 1)

                    return [lambda: tops(0), lambda: tops(8), pairs, lambda: topis(0), lambda: topis(8), bests,
                            scale, bestis, ranks, lambda: lookup(0), lambda: lookup(1), table]

                def empty_tab(i, w, first):
                    if not first:
                        dve.wait_ge(st_tab[w], 16 * i)
                    dve.wait_ge(aux_full, NU * i + UI[f"tab{w}"] + 1)
                    src = bank(f"tab{w}")[:, 0:3 * P].rearrange("p (a t) -> p a t", a=3)
                    dve.tensor_copy(tabT[0:64, w], src[0:64, :, 0:64])
                    dve.tensor_copy(tabT[64:128, w], src[64:128, :, 64:128]).then_inc(aux_dve, 1)

                def oT_lo(b, count, m, done):
                    dve.wait_ge(oT_hi, count)
                    half = slice(4 * m, 4 * m + 4)
                    dve.tensor_tensor(out=oT_l[:, half], in0=b, in1=oT_h[:, half].bitcast(F32),
                                      op=ALU.subtract).then_inc(done, 1)

                def add_x(i, w, b, first):
                    if not first:
                        dve.wait_ge(st_y[w], 16 * i)
                    dve.tensor_tensor(out=y[:, w], in0=b[:, 0:D], in1=xres[:, w], op=ALU.add).then_inc(aux_dve, 1)

                def body(i, first, own):
                    later = []
                    if not first:
                        wait_emptied(dve, i - 1, "sc3")
                        dve.wait_ge(tab_ready, W * i)
                        dve.memset(spare[:], 0.0)
                        for n, piece in enumerate(choose(W * i - W, 0)):
                            piece()
                            if n == 0 or n == 2:
                                oT_lo(ptb[:], 4 * i - 1 + n // 2, n // 2, late_lo)
                            if n == WO1_AFTER:
                                dve.wait_ge(aux_full, NU * i + UI["wo1"] + 1)
                                add_x(i, 1, bank("wo1"), False)
                        later = choose(W * i - W + 1, 1)

                    def maxima(n):
                        dve.wait_ge(qk_done, NG * i + n + 1)
                        dve.tensor_reduce(out=negmax[:, n], in_=sim[n % 2][:, :, 0:2 * KJ].rearrange(
                            "p e (j k) -> p e j k", k=KJ), axis=AX.X, op=ALU.max, negate=True).then_inc(max_done, 1)

                    def empty_pm(half):
                        dve.wait_ge(aux_full, NU * i + UI[f"pm{half}"] + 1)
                        src = bank(f"pm{half}")[:, 0:P]
                        dve.tensor_copy(pmT_h[:, half % 2], src).then_inc(pm_hi, 1)
                        dve.wait_ge(pm_hi, 4 * i + half + 1)
                        dve.tensor_tensor(out=pmT_l[:, half % 2], in0=src, in1=pmT_h[:, half % 2].bitcast(F32),
                                          op=ALU.subtract).then_inc(aux_dve, 1)

                    def normalise(half):
                        dve.wait_ge(exp_done, NG * i + 2 * half + 2)
                        if half > 0 or not first:
                            dve.wait_ge(norm_done, 4 * i + half)
                        dve.reciprocal(recip[:], rowsum[:, 2 * half:2 * half + 2].rearrange("p a b -> p (a b)")
                                       ).then_inc(rcp, 1)
                        dve.wait_ge(rcp, 4 * i + half + 1)
                        dve.wait_ge(pv_done, 4 * i + half + 1)
                        dve.tensor_tensor(
                            out=o[:, (half % 2) * BANK:(half % 2 + 1) * BANK].rearrange("p (h d) -> p h d", d=DH),
                            in0=pvb[:].rearrange("p (h d) -> p h d", d=DH),
                            in1=recip[:].unsqueeze(2).broadcast_to([P, 8, DH]), op=ALU.mult).then_inc(norm_done, 1)

                    if later:
                        dve.wait_ge(tab_ready, W * i + 1)
                        dve.memset(spare[:], 0.0)
                        later[0]()
                    maxima(0)
                    share = (later[1:4], later[4:6], later[6:8], later[8:10], later[10:12], [], [], [])
                    for n in range(NG):
                        if n == 3:
                            dve.wait_ge(ln_bn, W * i + 2 * W)
                        if n + 1 < NG:
                            maxima(n + 1)
                        if n == 3:
                            aggregate()
                        if n == 1:
                            empty_tab(i, 0, first)
                        if n == 5:
                            empty_tab(i, 1, first)
                        if n == 7:
                            dve.wait_ge(st_z, 16 * i + 16)
                            for w in range(W):
                                dve.wait_ge(aux_full, NU * i + UI[f"zT{w}"] + 1)
                                split_z(w, bank(f"zT{w}"), W * i + W + w + 1, aux_dve)
                        if n % 2 == 1:
                            empty_pm(n // 2)
                        for piece in share[n][:-1]:
                            piece()
                        if n == 6:
                            for m in range(2):
                                oT_lo(bank(f"oT{m}")[:].rearrange("p (c t) -> p c t", c=4), 4 * i + 1 + m, m, aux_dve)
                        if n >= 2 and n % 2 == 0:
                            normalise(n // 2 - 1)
                        for piece in share[n][-1:]:
                            piece()
                        if n == 2:
                            moments(i + 1)
                        if n == 5:
                            normed(i + 1)
                    if own:
                        dve.wait_ge(tab_ready, W * i + W)
                        dve.memset(spare[:], 0.0)
                        own[0]()
                        own[1]()
                    for piece in own[2:3]:
                        piece()
                    normalise(3)
                    for piece in own[3:5]:
                        piece()
                    dve.wait_ge(d_xres, 16 * i + 16)
                    dve.wait_ge(aux_full, NU * i + UI["wo0"] + 1)
                    add_x(i, 0, bank("wo0"), first)

                moments(0)
                dve.wait_ge(ln_bn, W)
                aggregate()
                normed(0)
                setup()
                for w in range(W):
                    dve.wait_ge(set_ps, 8 + w)
                    split_z(w, aux[(7 + w) % 2], w + 1, set_ev)
                for n, (lo, rows, hi) in enumerate(((wout_l, wout, wout_h), (pmv_l, pmv_bd, pmv_h))):
                    dve.wait_ge(split_hi, n + 1)
                    dve.tensor_tensor(out=lo[:], in0=rows[:], in1=hi[:].bitcast(F32),
                                      op=ALU.subtract).then_inc(split_lo, 1)
                dve.wait_ge(c_iota, 1)
                body(0, True, [])
                with dve.Fori(1, NI - 1) as i:
                    body(i, False, [])
                own = choose(W * (NI - 1), 0)
                body(NI - 1, False, own[:5])
                for m in range(2):
                    oT_lo(ptb[:], 4 * NI - 1 + m, m, late_lo)
                    for piece in own[5 + 2 * m:7 + 2 * m]:
                        piece()
                for piece in own[9:]:
                    piece()
                dve.wait_ge(aux_full, NU * NI + 1)
                add_x(NI, 1, aux[0], False)
                dve.wait_ge(tab_ready, W * NI + 1)
                dve.memset(spare[:], 0.0)
                for piece in choose(W * NI - 1, 1):
                    piece()
                for w in range(W):
                    dve.wait_ge(st_tab[w], 16 * NI)
                    dve.wait_ge(aux_full, NU * NI + w + 2)
                    src = aux[1 - w][:, 0:3 * P].rearrange("p (a t) -> p a t", a=3)
                    dve.tensor_copy(tabT[0:64, w], src[0:64, :, 0:64])
                    dve.tensor_copy(tabT[64:128, w], src[64:128, :, 64:128]).then_inc(aux_dve, 1)

            @block.tensor
            def _(pe):
                pe.wait_ge(c_ident, 2)
                pe.wait_ge(d_small, 16 * 4)
                for half in range(2):
                    last = pe.transpose(aux[0][:, half * P:(half + 1) * P], pmk2[:, half], ident[:])
                last.then_inc(set_ps, 1)
                pe.wait_ge(d_wq, 16 * 3)
                keyrows = raw[0:NK, KD * 3 * INNER:].rearrange("p (m d) -> p m d", d=DK)
                for n in range(2):
                    if n == 1:
                        pe.wait_ge(set_ev, 1)
                    for m in range(8):
                        last = pe.transpose(aux[(1 + n) % 2][:, m * NK:(m + 1) * NK], keyrows[:, 8 * n + m],
                                            ident[0:NK, 0:NK])
                    last.then_inc(set_ps, 1)
                for k in range(KD):
                    for n in range(2):
                        u = 3 + 2 * k + n
                        pe.wait_ge(set_ev, 3 if u == 3 else u - 1)
                        rows = (v if n == 0 else sc)[:].rearrange("p w (m d) -> p (w m) d", d=D)
                        for m in range(8):
                            last = pe.matmul(aux[u % 2][:, m * NK:(m + 1) * NK], rows[:, m, k * P:(k + 1) * P],
                                             o[:, (8 * n + m) * NK:(8 * n + m + 1) * NK], start=True, stop=True)
                        last.then_inc(set_ps, 1)
                pe.wait_ge(z_ready, W)
                for w in range(W):
                    pe.wait_ge(set_ev, 6 + w)
                    for k in range(KD):
                        last = pe.transpose(aux[(7 + w) % 2][:, k * P:(k + 1) * P], z[:, w, k * P:(k + 1) * P], ident[:])
                    last.then_inc(set_ps, 1)
                pe.wait_ge(set_ev, 9)
                pe.wait_ge(w_split, KD)
                pe.wait_ge(c_mask, 4)

                def use(i, name, first):
                    u = UI[name]
                    if u >= 2:
                        if not (first and USES[u - 2][0] == "wo1"):
                            wait_emptied(pe, i, USES[u - 2][0])
                    elif not first:
                        wait_emptied(pe, i - 1, USES[u - 2][0])
                    return bank(name)

                def transpose_o(m, b):
                    for c in range(4):
                        cc = 4 * (m % 2) + c
                        last = pe.transpose(b[:, c * P:(c + 1) * P], o[:, cc * P:(cc + 1) * P], ident[:])
                    return last

                def late_o(i, m):
                    pe.wait_ge(norm_done, 4 * i - 1 + m)
                    if m == 0:
                        pe.wait_ge(pt_ev, NG * i)
                    else:
                        pe.wait_ge(late_lo, 2 * i - 1)
                    transpose_o(m, ptb[:].rearrange("p c t -> p (c t)")).then_inc(late_full, 1)

                def project(b):
                    for c in range(CH):
                        last = split3(pe, b[:, 0:D], oT_h[:, c], oT_l[:, c], wout_h[:, c], wout_l[:, c], c == 0,
                                      c == CH - 1)
                    last.then_inc(aux_full, 1)

                def body(i, first):
                    if not first:
                        late_o(i, 0)
                        wait_emptied(pe, i - 1, "zT1")

                    def transpose_z():
                        pe.wait_ge(z_ready, W * i + 2 * W)
                        for w in range(W):
                            b = use(i, f"zT{w}", first)
                            for k in range(KD):
                                last = pe.transpose(b[:, k * P:(k + 1) * P], z[:, w, k * P:(k + 1) * P], ident[:])
                            last.then_inc(aux_full, 1)

                    for m in range(8):
                        b = use(i, f"qk{m}", first)
                        for c in range(2):
                            cols = slice((2 * m + c) * P, (2 * m + c + 1) * P)
                            for k in range(KD):
                                last = split3(pe, b[:, c * BLK:(c + 1) * BLK], wqkv_h[:, k, cols], wqkv_l[:, k, cols],
                                              zhl[:, 0, k], zhl[:, 1, k], k == 0, k == KD - 1)
                        last.then_inc(aux_full, 2 if first and m == 3 else 1)
                        if m == 1 and not first:
                            late_o(i, 1)
                        if m == 3 and not first:
                            b = use(i, "wo1", False)
                            pe.wait_ge(late_lo, 2 * i)
                            project(b)

                    def rows_times(name, wh, wl, w, n0):
                        b = use(i, name, first)
                        tok = slice(w * P, (w + 1) * P)
                        for k in range(KD):
                            last = split3(pe, b[:], zhl[:, 0, k, tok], zhl[:, 1, k, tok], wh[:, k, n0:n0 + BANK],
                                          wl[:, k, n0:n0 + BANK], k == 0, k == KD - 1)
                        last.then_inc(aux_full, 1)

                    def values(m):
                        rows_times(f"v{m}", wqkv_h, wqkv_l, m // 2, 2 * INNER + (m % 2) * BANK)

                    values(0)
                    values(1)

                    def scores(m):
                        rows_times(f"sc{m}", wsc_h, wsc_l, m // 2, (m % 2) * BANK)

                    def qk(n):
                        w = n // 4
                        if n >= 2:
                            pe.wait_ge(exp_done, NG * i + n - 1)
                        elif not first:
                            pe.wait_ge(exp_done, NG * i + n - 1)
                        if n == 0:
                            wait_emptied(pe, i, "qk7")
                        for par in range(2):
                            pe.matmul(sim[n % 2][:, par, 0:2 * KJ].rearrange("p (j k) -> p j k", k=KJ), identb[:],
                                      maskneg[:].unsqueeze(1).broadcast_to([P, 2, KJ]), start=True, stop=False)
                        for j in range(2):
                            for par in range(2):
                                c = 2 * (n % 4) + j
                                rows = slice(par * DH, (par + 1) * DH)
                                last = pe.matmul(sim[n % 2][:, par, j * KJ:(j + 1) * KJ],
                                                 qT[rows, c, w * P:(w + 1) * P], kT[rows, c, w, :],
                                                 start=False, stop=(j == 1))
                        last.then_inc(qk_done, 1)

                    def transpose_probs(n):
                        pe.wait_ge(exp_done, NG * i + n + 1)
                        if n >= 1:
                            pe.wait_ge(pt_ev, NG * i + n)
                        elif not first:
                            pe.wait_ge(late_lo, 2 * i)
                        for hh in range(4):
                            last = pe.transpose(ptb[:, hh], prob[n // 2 % 2][:, 4 * (n % 2) + hh, PM:KJ], ident[:])
                        last.then_inc(pt_done, 1)

                    def transpose_pm(half):
                        b = use(i, f"pm{half}", first)
                        pe.wait_ge(pm_packed, 4 * i + half + 1)
                        pe.transpose(b[:, 0:P], probpm[:, half % 2].rearrange("p h s -> p (h s)"),
                                     ident[:]).then_inc(aux_full, 1)

                    def pv(n):
                        half = n // 2
                        if n % 4 == 0:
                            wait_emptied(pe, i, f"v{n // 4 * 2 + 1}")
                        if n % 2 == 0 and (half > 0 or not first):
                            pe.wait_ge(norm_done, 4 * i + half)
                        pe.wait_ge(pt_ev, NG * i + n + 1)
                        for hh in range(4):
                            head = 4 * (n % 4) + hh
                            slot = 4 * (n % 2) + hh
                            pe.matmul(pvb[:, slot * DH:(slot + 1) * DH], probT[n % 2][:, hh],
                                      v[:, n // 4, head * DH:(head + 1) * DH], start=(slot == 0), stop=False)
                        if n % 2 == 1:
                            wait_emptied(pe, i, f"pm{half}")
                            if n == 1 and first:
                                pe.wait_ge(split_lo, 2)
                            split3(pe, pvb[:], pmT_h[:, half % 2], pmT_l[:, half % 2], pmv_h[:, half % 2],
                                   pmv_l[:, half % 2], False, True).then_inc(pv_done, 1)

                    def transpose_tab(w):
                        b = use(i, f"tab{w}", first)
                        pe.wait_ge(tab_ready, W * i + w + 1)
                        for a in range(3):
                            last = pe.transpose(b[:, a * P:(a + 1) * P], tab[:, w, a].rearrange("p e c -> p (e c)"),
                                                ident[:])
                        last.then_inc(aux_full, 1)

                    qk(0)
                    for n in range(NG):
                        if n + 1 < NG:
                            qk(n + 1)
                        if n == 0:
                            values(2)
                            values(3)
                        if n == 1:
                            transpose_tab(0)
                        if 2 <= n < 6:
                            scores(n - 2)
                        if n == 6:
                            for m in range(2):
                                b = use(i, f"oT{m}", first)
                                pe.wait_ge(norm_done, 4 * i + m + 1)
                                transpose_o(m, b).then_inc(aux_full, 1)
                        if n == 7:
                            transpose_z()
                        transpose_probs(n)
                        if n % 2 == 1:
                            pv(n - 1)
                            if n == 5:
                                transpose_tab(1)
                            transpose_pm(n // 2)
                        elif n >= 1:
                            pv(n - 1)
                    pv(7)
                    b = use(i, "wo0", first)
                    wait_emptied(pe, i, "oT1")
                    project(b)

                body(0, True)
                with pe.Fori(1, NI) as i:
                    body(i, False)
                for m in range(2):
                    late_o(NI, m)
                wait_emptied(pe, NI - 1, USES[NU - 2][0])
                pe.wait_ge(late_lo, 2 * NI)
                project(aux[0])
                wait_emptied(pe, NI - 1, USES[NU - 1][0])
                for w in range(W):
                    if w == 1:
                        pe.wait_ge(aux_dve, ND * NI + 1)
                    pe.wait_ge(tab_ready, W * NI + w + 1)
                    for a in range(3):
                        last = pe.transpose(aux[1 - w][:, a * P:(a + 1) * P], tab[:, w, a].rearrange("p e c -> p (e c)"),
                                            ident[:])
                    last.then_inc(aux_full, 1)

        with ExitStack() as ctx:
            def sb(name, shape, dt):
                return ctx.enter_context(nc.sbuf_tensor(name, shape, dt))

            def ps(name, shape, dt=F32):
                return ctx.enter_context(nc.psum_tensor(name, shape, dt))

            UQ = 32
            NUN = BLK // 2 // UQ
            PC = 8
            NP = BLK // 2 // PC
            ND2 = LO // 2

            wd_h = sb("wd_h", [P, LO, KD, P], F32R)
            wd_l = sb("wd_l", [P, LO, KD, P], F32R)
            g = early[:].rearrange("p (s c t) -> p s c t", s=W + 1, t=P)
            iota = sb("iota", [P, P, UQ], BF16)
            hmask = sb("hmask", [P, 2], F32)
            left = [sb(f"left{n}", [P, P, UQ], BF16) for n in range(2)]
            onehot = sb("onehot", [P, LO, UQ], F16)
            right = [sb(f"right{n}", [P, 2, LO, 2, UQ], F16) for n in range(2)]
            tb = sb("tb", [P, W, 3, NC], F32)
            ids = sb("ids", [P, 2, W, NC], BF16)
            part = sb("part", [P, 2, W, NC], F16)
            wpart = sb("wpart", [P, 2, 2, W, NC], F16)
            zb = sb("zb", [P, 2, KD, BLK], F32R)
            yb = sb("yb", [P, W, D], F32)
            res = sb("res", [P, W, D], F32)

            dps = [ps(f"dps{n}", [P, 2, BLK]) for n in range(2)]
            cps = [ps(f"cps{n}", [P, PC, LO, 2]) for n in range(3)]
            ups = [ps(f"ups{n}", [P, BANK]) for n in range(2)]

            c_iotab = sem("c_iotab")
            dt_ps = sem("dt_ps")
            dt_hi = sem("dt_hi")
            dt_ev = sem("dt_ev")
            d_zb = sem("d_zb")
            d_tb = sem("d_tb")
            d_yb = [sem(f"d_yb{w}") for w in range(W)]
            st_out = [sem(f"st_out{w}") for w in range(W)]
            p_ids = sem("p_ids")
            p_step = sem("p_step")
            p_w = sem("p_w")
            u_one = sem("u_one")
            u_ready = sem("u_ready")
            down_done = sem("down_done")
            gelu_done = sem("gelu_done")
            c_done = sem("c_done")
            mul_done = sem("mul_done")
            up_done = [sem(f"up_done{w}") for w in range(W)]
            add_done = [sem(f"add_done{w}") for w in range(W)]

            turn = [c[:].rearrange("p q c e -> p (q c e)") for c in cps] + [b[:] for b in ups]
            NT = LO * KD // 4

            def slots(par):
                return g[:, 0:2 + par:1 + par]

            block = ctx.enter_context(nc.Block())

            @block.sync
            def _(sp):
                def body(i, first):
                    if not first:
                        sp.wait_ge(p_w, i)
                    for w in range(W):
                        sp.dma_start(tb[:, w].rearrange("p a q -> p (a q)"),
                                     tab_scratch[W * i + W + w]).then_inc(d_tb, 16)
                    if not first:
                        sp.wait_ge(down_done, ND2 * i)
                    sp.dma_start(zb[:].rearrange("p a k t -> p (a k t)").bitcast(F32), z_scratch[i]).then_inc(d_zb, 16)
                    if first:
                        sp.dma_start(upw[:], expert_up.rearrange("(p c) d -> p c d", c=LO)).then_inc(d_up, 16)
                    if not first:
                        store(i - 1, 0)
                    load_y(i, 0)
                    if not first:
                        store(i - 1, 1)
                    load_y(i, 1)

                def load_y(i, w):
                    sp.dma_start(yb[:, w], out_blk[i, :, w]).then_inc(d_yb[w], 16)

                def store(i, w):
                    sp.wait_ge(add_done[w], i + 1)
                    sp.dma_start(out_blk[i, :, w], res[:, w]).then_inc(st_out[w], 16)

                body(0, True)
                with sp.Fori(1, NI) as i:
                    body(i, False)
                for w in range(W):
                    store(NI - 1, w)
                for w in range(W):
                    sp.wait_ge(st_out[w], 16 * NI)

            @block.gpsimd
            def _(pool):
                pool.iota(iota[:], pattern=[[1, P], [0, UQ]], base=0, channel_multiplier=0,
                          allow_small_or_imprecise_dtypes=True).then_inc(c_iotab, 1)
                pool.memset(hmask[:], 1.0).then_inc(c_iotab, 1)
                pool.wait_ge(c_iotab, 2)
                pool.affine_select(out=hmask[:, 0:1], in_=hmask[:, 0:1], compare_op=ALU.is_ge, fill=0.0, base=63,
                                   pattern=[[0, 1]], channel_multiplier=-1).then_inc(c_iotab, 1)
                pool.affine_select(out=hmask[:, 1:2], in_=hmask[:, 1:2], compare_op=ALU.is_ge, fill=0.0, base=-64,
                                   pattern=[[0, 1]], channel_multiplier=1).then_inc(c_iotab, 1)

            @block.scalar
            def _(act):
                act.preload_act_table(ACT.Gelu)
                for u in range(NT):
                    k, c0 = u % KD, 4 * (u // KD)
                    act.wait_ge(dt_ps, u + 1)
                    act.activation(wd_h[:, c0:c0 + 4, k], turn[u % len(turn)].rearrange("p (c e) -> p c e", c=4), ACT.Copy, scale=nrm[:, k:k + 1]).then_inc(dt_hi, 1)

                def body(i, par):
                    for m in range(ND2):
                        act.wait_ge(down_done, ND2 * i + m + 1)
                        act.activation(slots(par)[:, :, 2 * m:2 * m + 2].rearrange("p w c t -> p c w t"),
                                       dps[m % 2][:].rearrange("p c (w t) -> p c w t", w=W),
                                       ACT.Gelu).then_inc(gelu_done, 1)

                for i in range(2):
                    body(i, i)
                with act.Fori(1, NI // 2) as j:
                    for par in range(2):
                        body(2 * j + par, par)

            @block.vector
            def _(dve):
                for u in range(NT):
                    k = u % KD
                    c0 = 4 * (u // KD)
                    src = turn[u % len(turn)].rearrange("p (c e) -> p c e", c=4)
                    dve.wait_ge(dt_hi, u + 1)
                    dve.scalar_tensor_tensor(out=wd_l[:, c0:c0 + 4, k], in0=src, scalar=nrm[:, k:k + 1],
                                             in1=wd_h[:, c0:c0 + 4, k].bitcast(F32), op0=ALU.mult,
                                             op1=ALU.subtract).then_inc(dt_ev, 1)
                dve.wait_ge(c_iotab, 4)

                def prepare(i, first):
                    b = 2 * i
                    dve.wait_ge(d_tb, 16 * W * i + 16 * W)
                    if not first:
                        dve.wait_ge(u_ready, NUN * i)
                    for a in range(2):
                        last = dve.tensor_copy(ids[:, a], tb[:, :, a])
                    last.then_inc(p_ids, 1)
                    wt = tb[:, :, 2]
                    dve.tensor_copy(part[:, 0], wt).then_inc(p_step, 1)
                    dve.wait_ge(p_step, b + 1)
                    dve.tensor_tensor(out=part[:, 1], in0=wt, in1=part[:, 0], op=ALU.subtract).then_inc(p_step, 1)
                    dve.wait_ge(p_step, b + 2)
                    for half in range(2):
                        last = dve.tensor_scalar(out=wpart[:, :, half], in0=part[:], scalar1=hmask[:, half:half + 1],
                                                 scalar2=None, op0=ALU.mult)
                    last.then_inc(p_w, 1)

                def build(i, u, first):
                    w, q0 = u // 2, (u % 2) * UQ

                    def left_rows():
                        if u == 0:
                            dve.wait_ge(p_ids, i + 1)
                            dve.wait_ge(p_w, i + 1)
                        if u >= 2 or not first:
                            dve.wait_ge(c_done, NP * i + 4 * u - 4)
                        dve.tensor_tensor(out=left[u % 2][:],
                                          in0=ids[:, 0, w, q0:q0 + UQ].unsqueeze(1).broadcast_to([P, P, UQ]),
                                          in1=iota[:], op=ALU.is_equal)

                    def onehot_rows():
                        if u > 0:
                            dve.wait_ge(u_ready, NUN * i + u)
                        dve.tensor_tensor(out=onehot[:],
                                          in0=ids[:, 1, w, q0:q0 + UQ].unsqueeze(1).broadcast_to([P, LO, UQ]),
                                          in1=iota[:, 0:LO], op=ALU.is_equal).then_inc(u_one, 1)

                    def right_rows(s):
                        dve.wait_ge(u_one, NUN * i + u + 1)
                        ins = dve.tensor_tensor(
                            out=right[u % 2][:, s], in0=onehot[:].unsqueeze(2).broadcast_to([P, LO, 2, UQ]),
                            in1=wpart[:, s, :, w, q0:q0 + UQ].unsqueeze(1).broadcast_to([P, LO, 2, UQ]), op=ALU.mult)
                        if s == 1:
                            ins.then_inc(u_ready, 1)

                    return [left_rows, onehot_rows, lambda: right_rows(0), lambda: right_rows(1)]

                def times_c(i, par, n):
                    w, q0 = n // 8, (n % 8) * PC
                    if n == 0:
                        dve.wait_ge(gelu_done, ND2 * i + ND2)
                    dve.wait_ge(c_done, NP * i + n + 1)
                    tok = slots(par)[:, w].rearrange("p c (e q) -> p c e q", e=2)
                    for half in range(2):
                        gv = tok[:, :, half, q0:q0 + PC]
                        last = dve.tensor_tensor(out=gv, in0=cps[n % 3][:, :, :, half].rearrange("p q c -> p c q"),
                                                 in1=gv, op=ALU.mult)
                    last.then_inc(mul_done, 1)

                def finish(i, w, first):
                    dve.wait_ge(d_yb[w], 16 * i + 16)
                    if not first:
                        dve.wait_ge(st_out[w], 16 * i)
                    dve.wait_ge(up_done[w], i + 1)
                    dve.scalar_tensor_tensor(out=res[:, w], in0=ups[w][:, 0:D], scalar=unscale[:, bass.ds(W * i + w, 1)],
                                             in1=yb[:, w], op0=ALU.mult, op1=ALU.add).then_inc(add_done[w], 1)

                def body(i, par, first):
                    prepare(i, first)
                    for step in build(i, 0, first) + build(i, 1, first):
                        step()
                    steps = {}
                    for u in range(2, NUN):
                        for m, step in enumerate(build(i, u, first)):
                            steps[4 * u - 5 + m] = step
                    for n in range(NP):
                        times_c(i, par, n)
                        if n in steps:
                            steps[n]()
                        if n == 9 and not first:
                            finish(i - 1, 1, isinstance(i, int) and i == 1)
                    finish(i, 0, first)

                for i in range(2):
                    body(i, i, i == 0)
                with dve.Fori(1, NI // 2) as j:
                    for par in range(2):
                        body(2 * j + par, par, False)
                finish(NI - 1, 1, False)

            @block.tensor
            def _(pe):
                pe.wait_ge(d_down, 16)
                for u in range(NT):
                    k = u % KD
                    c0 = 4 * (u // KD)
                    dst = turn[u % len(turn)]
                    if u >= len(turn):
                        pe.wait_ge(dt_ev, u - len(turn) + 1)
                    for c in range(4):
                        last = pe.transpose(dst[:, c * P:(c + 1) * P], down_raw[:, c0 + c, k * P:(k + 1) * P], ident[:])
                    last.then_inc(dt_ps, 1)

                def c_piece(i, n, first):
                    if n % 4 == 0:
                        pe.wait_ge(u_ready, NUN * i + n // 4 + 1)
                    if n >= 3 or not first:
                        pe.wait_ge(mul_done, NP * i + n - 2)
                    u, pc = n // 4, n % 4
                    for q in range(PC):
                        for s in range(2):
                            last = pe.matmul(cps[n % 3][:, q], left[u % 2][:, :, pc * PC + q],
                                             right[u % 2][:, s, :, :, pc * PC + q],
                                             start=(s == 0), stop=(s == 1))
                    last.then_inc(c_done, 1)

                def up(i, par, w, c0, n, first):
                    if c0 == 0:
                        pe.wait_ge(mul_done, NP * i + 8 * w + 8)
                        if w == 0 and first:
                            pe.wait_ge(d_up, 16)
                        if not first:
                            pe.wait_ge(add_done[w], i)
                    for c in range(c0, c0 + n):
                        last = pe.matmul(ups[w][:, 0:D], slots(par)[:, w, c], upw[:, c],
                                         start=(c == 0), stop=(c == LO - 1))
                    if c0 + n == LO:
                        last.then_inc(up_done[w], 1)

                def body(i, par, first):
                    pe.wait_ge(d_zb, 16 * i + 16)
                    for m in range(ND2):
                        if first:
                            pe.wait_ge(dt_ev, 2 * (m // 2) + 2)
                        if m >= 2 or not first:
                            pe.wait_ge(gelu_done, ND2 * i + m - 1)
                        for c in range(2):
                            for k in range(KD):
                                last = split3(pe, dps[m % 2][:, c], wd_h[:, 2 * m + c, k], wd_l[:, 2 * m + c, k],
                                              zb[:, 0, k], zb[:, 1, k], k == 0, k == KD - 1)
                        last.then_inc(down_done, 1)
                    for n in range(8):
                        c_piece(i, n, first)
                        if not first:
                            up(i - 1, 1 - par, 1, 4 * n, 4, isinstance(i, int) and i == 1)
                    c_piece(i, 8, first)
                    for n in range(8):
                        up(i, par, 0, 4 * n, 4, first)
                        if n < 7:
                            c_piece(i, 9 + n, first)

                for i in range(2):
                    body(i, i, i == 0)
                with pe.Fori(1, NI // 2) as j:
                    for par in range(2):
                        body(2 * j + par, par, False)
                up(NI - 1, 1, 1, 0, LO, False)


_INS = ['L0_attn_x', 'L0_attn_gamma', 'L0_attn_w_qkv', 'L0_attn_w_out', 'L0_attn_pm_k', 'L0_attn_pm_v',
        'L0_ffn_w_q', 'L0_ffn_keys', 'L0_ffn_expert_down', 'L0_ffn_expert_up', 'L0_ffn_norm_w']


def kernel(**inputs):
    import numpy as np
    import concourse.bacc as bacc
    from concourse.bass_utils import run_bass_kernel_spmd

    nc = bacc.Bacc("TRN2", target_bir_lowering=False, num_devices=1)
    arrays, args = {}, []
    for name in _INS:
        a = np.ascontiguousarray(inputs[name])
        arrays[f"in_{name}"] = a
        args.append(nc.dram_tensor(f"in_{name}", a.shape, mybir.dt.from_np(a.dtype), kind="ExternalInput").ap())
    shape = arrays['in_L0_attn_x'].shape
    args.append(nc.dram_tensor("out_0", shape, F32, kind="ExternalOutput").ap())
    attention_experts(nc, *args)
    r = run_bass_kernel_spmd(nc, [arrays], core_ids=[0])
    return r.results[0]["out_0"]
```
